# Optimizing a Trainium2 kernel written in Bass

```python
import numpy as np
import jax
import jax.numpy as jnp

def _softmax(x, axis=-1):
    return jax.nn.softmax(x, axis=axis)

def _gelu(x):
    return jax.nn.gelu(x, approximate=True)

def _silu(x):
    return jax.nn.silu(x)

def _sigmoid(x):
    return jax.nn.sigmoid(x)

def _layernorm(x, axis=-1, eps=1e-05):
    m = jnp.mean(x, axis=axis, keepdims=True)
    v = jnp.var(x, axis=axis, keepdims=True)
    return (x - m) / jnp.sqrt(v + eps)

def _scatter_add(tgt, idx, src, axis=0):
    return tgt.at[idx].add(src)

def _segment_sum(src, seg, n):
    return jax.ops.segment_sum(src, seg, n)
kernel_name = 'mk_gnn_preln_d2_gnn_r8_5e7029'

def setup_inputs(seed: int=0):
    np.random.seed(seed)
    _w = jnp.asarray

    def _rec_inputs():
        import jax
        import jax.numpy as jnp
        _gk = jax.random.key(seed)
        x = -0.0001006 + 1 * jax.random.normal(jax.random.fold_in(_gk, 1), (12500, 48), jnp.float32)
        src = jax.random.randint(jax.random.fold_in(_gk, 2), (400000,), 0, 12500, jnp.int32)
        dst = jax.random.randint(jax.random.fold_in(_gk, 3), (400000,), 0, 12500, jnp.int32)
        _o = jnp.argsort(dst, stable=True)
        src = src[_o]
        dst = dst[_o]
        edge_attr_16 = 0.000196303 + 1.00016 * jax.random.normal(jax.random.fold_in(_gk, 11), (400000, 16), jnp.float32)
        return (x, src, dst, edge_attr_16)
    x, src, dst, edge_attr_16 = _rec_inputs()

    def _L0_gnn_setup():
        import jax, jax.numpy as jnp
        import numpy as np
        N_NODES = 12500
        N_EDGES = 200000
        IN_F = 48
        OUT_F = 48
        key = jax.random.key(seed)
        k1, k2, k3, k4 = jax.random.split(key, 4)
        x = jax.random.normal(k1, (N_NODES, IN_F), dtype=jnp.float32)
        edge_index = jax.random.randint(k2, (2, N_EDGES), 0, N_NODES, dtype=jnp.int32)
        bound = 1.0 / np.sqrt(IN_F)
        W = jax.random.uniform(k3, (OUT_F, IN_F), minval=-bound, maxval=bound, dtype=jnp.float32)
        b = jax.random.uniform(k4, (OUT_F,), minval=-bound, maxval=bound, dtype=jnp.float32)
        return {'x': x, 'edge_index': edge_index, 'W': W, 'b': b}
    _L0_gnn_all = _L0_gnn_setup()
    _L0_gnn_in = {k: v for k, v in _L0_gnn_all.items() if k in ('W', 'b')}
    del _L0_gnn_all

    def _L1_gnn_setup():
        import jax, jax.numpy as jnp
        import numpy as np
        N_NODES = 12500
        N_EDGES = 200000
        N_FEAT = 48
        N_EDGE_FEAT = 16
        HIDDEN = 128
        key = jax.random.key(seed)
        ks = jax.random.split(key, 8)
        tot = 2 * N_FEAT + N_EDGE_FEAT
        s1 = 1.0 / np.sqrt(tot)
        s2 = 1.0 / np.sqrt(HIDDEN)
        return {'x': jax.random.normal(ks[0], (N_NODES, N_FEAT), dtype=jnp.float32), 'edge_index': jax.random.randint(ks[1], (2, N_EDGES), 0, N_NODES, dtype=jnp.int64), 'edge_feat': jax.random.normal(ks[2], (N_EDGES, N_EDGE_FEAT), dtype=jnp.float32), 'W1': jax.random.normal(ks[3], (tot, HIDDEN), dtype=jnp.float32) * s1, 'b1': jnp.zeros((HIDDEN,), dtype=jnp.float32), 'W2': jax.random.normal(ks[4], (HIDDEN, HIDDEN), dtype=jnp.float32) * s2, 'b2': jnp.zeros((HIDDEN,), dtype=jnp.float32), 'W3': jax.random.normal(ks[5], (HIDDEN, N_FEAT), dtype=jnp.float32) * s2, 'b3': jnp.zeros((N_FEAT,), dtype=jnp.float32)}
    _L1_gnn_all = _L1_gnn_setup()
    _L1_gnn_in = {k: v for k, v in _L1_gnn_all.items() if k in ('W1', 'b1', 'W2', 'b2', 'W3', 'b3')}
    del _L1_gnn_all
    return {'x': x, 'src': src, 'dst': dst, 'edge_attr_16': edge_attr_16, 'L0_gnn_W': _L0_gnn_in['W'], 'L0_gnn_b': _L0_gnn_in['b'], 'L1_gnn_W1': _L1_gnn_in['W1'], 'L1_gnn_b1': _L1_gnn_in['b1'], 'L1_gnn_W2': _L1_gnn_in['W2'], 'L1_gnn_b2': _L1_gnn_in['b2'], 'L1_gnn_W3': _L1_gnn_in['W3'], 'L1_gnn_b3': _L1_gnn_in['b3']}

def reference(x, src, dst, edge_attr_16, L0_gnn_W, L0_gnn_b, L1_gnn_W1, L1_gnn_b1, L1_gnn_W2, L1_gnn_b2, L1_gnn_W3, L1_gnn_b3):
    import jax
    import jax.numpy as jnp

    def _L0_gnn_ref(x, edge_index, W, b):
        import jax, jax.numpy as jnp
        import numpy as np
        N_NODES = 12500
        N_EDGES = 200000
        IN_F = 48
        OUT_F = 48
        row, col = (edge_index[0], edge_index[1])
        n = x.shape[0]
        deg = jnp.bincount(row, length=n).astype(x.dtype)
        deg_inv_sqrt = jnp.where(deg > 0, jax.lax.rsqrt(jnp.where(deg > 0, deg, 1.0)), 0.0)
        norm = deg_inv_sqrt[row] * deg_inv_sqrt[col]
        msg = norm[:, None] * x[col]
        agg = jax.ops.segment_sum(msg, row, num_segments=n)
        out = agg @ W.T + b
        return jax.nn.relu(out)

    def _L1_gnn_ref(x, edge_index, edge_feat, W1, b1, W2, b2, W3, b3):
        import jax, jax.numpy as jnp
        import numpy as np
        N_NODES = 12500
        N_EDGES = 200000
        N_FEAT = 48
        N_EDGE_FEAT = 16
        HIDDEN = 128
        source = edge_index[0]
        target = edge_index[1]
        edge = jnp.concatenate([x[source], x[target], edge_feat], axis=-1)
        h = jax.nn.relu(edge @ W1 + b1)
        h = jax.nn.relu(h @ W2 + b2)
        message = h @ W3 + b3
        n = x.shape[0]
        msum = jax.ops.segment_sum(message, target, num_segments=n)
        cnt = jax.ops.segment_sum(jnp.ones((target.shape[0],), dtype=x.dtype), target, num_segments=n)
        update = msum / jnp.maximum(cnt, 1.0)[:, None]
        return x + update
    edge_index = jnp.stack([src, dst])
    h = jnp.maximum(_layernorm(x, axis=-1), 0.0)
    x = x + _L0_gnn_ref(h, edge_index, L0_gnn_W, L0_gnn_b)
    h = jnp.maximum(_layernorm(x, axis=-1), 0.0)
    x = x + _L1_gnn_ref(h, edge_index, edge_attr_16, L1_gnn_W1, L1_gnn_b1, L1_gnn_W2, L1_gnn_b2, L1_gnn_W3, L1_gnn_b3)
    return x

_drawn_inputs = setup_inputs


def setup_inputs(seed=0):
    import zlib

    import numpy as np

    out = dict(_drawn_inputs(seed))
    spreads = {'L1_gnn_b1': (0.0, 0.338), 'L1_gnn_b2': (0.0, 0.1), 'L1_gnn_b3': (0.0, 0.1)}
    factors = {'edge_attr_16': 3.114}
    for name, (base, spread) in spreads.items():
        noise = np.random.default_rng([zlib.crc32(name.encode()), seed]).standard_normal(out[name].shape)
        drawn = base * np.exp(spread * noise) if base else spread * noise
        out[name] = jnp.asarray(drawn.astype(out[name].dtype))
    for name, factor in factors.items():
        out[name] = (out[name] * factor).astype(out[name].dtype)
    return out
```

```python
from contextlib import ExitStack

import concourse.bass as bass
from concourse import mybir

P = 128
GROUP = 4
TABLES = GROUP
PLANES = 3
PAD_NODE = 1 << 20
EPS = 1e-5

ALU = mybir.AluOpType
ACT = mybir.ActivationFunctionType
AX = mybir.AxisListType
F32 = mybir.dt.float32
BF16 = mybir.dt.bfloat16
I32 = mybir.dt.int32


def divisor(n, most):
    return max(d for d in range(1, most + 1) if n % d == 0)


def build_gnn(nc, x, src_col, dst_col, dst_row, edge_t, w0_t, b0, w1ab, w1c, b1, w2, b2, w3, b3, out):
    N, F = out.shape
    NB = x.shape[0] // P
    NP = NB * P
    TP = src_col.shape[1]
    T = dst_row.shape[0]
    EF = edge_t.shape[0]
    H = w2.shape[0]
    MOST = -(-T // GROUP) + 1
    CB = divisor(NB, 7)
    NK = NB // CB
    HC = divisor(T, 25)
    SP_, SK = divisor(T, P), T // divisor(T, P)
    W = GROUP * P
    assert TP >= GROUP * MOST and H == P

    sum_tab = [nc.dram_tensor(f"sum_tab{j}", [NP + P, F], F32).ap() for j in range(TABLES)]
    p_tab = nc.dram_tensor("p_tab", [NP, PLANES * H], BF16).ap()
    ext_tab = nc.dram_tensor("ext_tab", [2, T], F32).ap()

    def node_view(table):
        return table[0:NP, :].rearrange("(b p) f -> p b f", p=P)

    with ExitStack() as whole:
        def sb(name, shape, dt, ctx=whole):
            return ctx.enter_context(nc.sbuf_tensor(name, shape, dt))

        def ps(name, shape, dt, ctx):
            return ctx.enter_context(nc.psum_tensor(name, shape, dt))

        def sem(name, ctx=whole):
            return ctx.enter_context(nc.semaphore(name))

        src_i = sb("src_i", [P, TP], I32)
        src_f = sb("src_f", [P, TP], F32)
        dst_f = sb("dst_f", [P, TP], F32)
        x1 = sb("x1", [P, NB, F], F32)
        act_in = sb("act_in", [P, NB, F], F32)
        sched = sb("sched", [1, 3 * NB + 1], I32)
        node_id = sb("node_id", [P, NB], F32)
        block_base = sb("block_base", [P, NB], F32)
        iota_row = sb("iota_row", [P, P], F32)
        ident_f = sb("ident_f", [P, P], F32)
        ident_b = sb("ident_b", [P, P], BF16)
        below = sb("below", [P, P], F32)
        above = sb("above", [P, P], F32)
        trash = sb("trash", [P, 1], F32)
        deg_is = sb("deg_is", [P, NB], F32)
        dst_cnt = sb("dst_cnt", [P, NB], F32)
        half = sb("half", [P, NB], F32)
        stat = sb("stat", [P, NB], F32)

        def layer_norm(dve, link, pool_pow, a, scratch):
            link(dve.tensor_reduce(stat[:, :], a, AX.X, ALU.add))
            link(dve.tensor_scalar(stat[:, :], stat[:, :], 1.0 / F, None, ALU.mult))
            link(dve.tensor_tensor(act_in[:, :, :], a, stat[:, :].unsqueeze(2).to_broadcast([P, NB, F]), ALU.subtract))
            link(dve.tensor_tensor(scratch, act_in[:, :, :], act_in[:, :, :], ALU.mult))
            link(dve.tensor_reduce(stat[:, :], scratch, AX.X, ALU.add))
            link(dve.tensor_scalar(stat[:, :], stat[:, :], 1.0 / F, EPS, ALU.mult, ALU.add))
            pool_pow()
            link(dve.tensor_tensor(act_in[:, :, :], act_in[:, :, :],
                                   stat[:, :].unsqueeze(2).to_broadcast([P, NB, F]), ALU.mult))
            link(dve.tensor_scalar(act_in[:, :, :], act_in[:, :, :], 0.0, None, ALU.max))

        def load_block(eng, b):
            first = eng.value_load(sched[0:1, bass.ds(b, 1)], min_val=0, max_val=TP - GROUP)
            groups = eng.value_load(sched[0:1, bass.ds(b + NB, 1)], min_val=1, max_val=MOST)
            before = eng.value_load(sched[0:1, bass.ds(b + 2 * NB, 1)], min_val=0, max_val=NB * MOST)
            return first, groups, before

        def tile_of(eng, first, i):
            return eng.snap(nc.s_assert_within(first + i * GROUP, 0, TP - GROUP))

        with ExitStack() as g_life:
            g_planes = sb("g_planes", [P, NB, PLANES, F], BF16, g_life)
            with ExitStack() as ctx:
                dst_i = sb("dst_i", [P, TP], I32, ctx)
                x_in = x1
                lo_b = sb("lo_b", [P, TP], BF16, ctx)
                hi_b = sb("hi_b", [P, TP], BF16, ctx)
                iota_b = sb("iota_b", [P, P], BF16, ctx)
                hot_lo = [sb(f"hot_lo{k}", [P, HC, P], BF16, ctx) for k in range(2)]
                hot_hi = [sb(f"hot_hi{k}", [P, HC, NB], BF16, ctx) for k in range(2)]
                scratch = sb("scratch", [P, NB, F], F32, ctx)
                zero_rows = scratch
                hist = ps("hist", [P, NB], F32, ctx)
                rows_ps = ps("rows_ps", [1, 3 * NB], F32, ctx)

                loaded = sem("loaded", ctx)
                x_loaded = sem("x_loaded", ctx)
                row_loaded = sem("row_loaded", ctx)
                const_ready = sem("const_ready", ctx)
                hot_ready = sem("hot_ready", ctx)
                hot_used = sem("hot_used", ctx)
                ext_ready = sem("ext_ready", ctx)
                ext_saved = sem("ext_saved", ctx)
                ext_loaded = sem("ext_loaded", ctx)
                runs_ready = sem("runs_ready", ctx)
                rows_ready = sem("rows_ready", ctx)
                zero_ready = sem("zero_ready", ctx)
                zeroed = sem("zeroed", ctx)
                hot_zero = sem("hot_zero", ctx)
                pow_ask = sem("pow_ask", ctx)
                pow_done = sem("pow_done", ctx)
                chain = sem("chain", ctx)
                pool_chain = sem("pool_chain", ctx)

                sched_ctx = ctx.enter_context(ExitStack())
                row_view = sb("row_view", [SP_, SK, P], I32, sched_ctx)
                tile_ext = sb("tile_ext", [SP_, 2, SK], F32, sched_ctx)
                ext_bc = g_planes[0:NB, :, :, :].rearrange("p b k f -> p (b k f)").bitcast(F32)[:, 0:2 * T]\
                    .rearrange("p (k t) -> p k t", k=2)
                tile_up = sb("tile_up", [NB, T], F32, sched_ctx)
                run = sb("run", [NB, 4], F32, sched_ctx)
                run_i = sb("run_i", [NB, 1], I32, sched_ctx)
                row = sb("row", [1, 4, NB], F32, sched_ctx)
                row_i = sb("row_i", [1, 2], I32, sched_ctx)
                bound = sb("bound", [NB, 2], F32, sched_ctx)

                block = ctx.enter_context(nc.Block())

                @block.sync
                def _(sp):
                    sp.dma_start(src_i[:, :], src_col).then_inc(loaded, 16)
                    sp.dma_start(dst_i[:, :], dst_col).then_inc(loaded, 16)
                    sp.dma_start(row_view[:, :, :], dst_row.rearrange("(p k) e -> p k e", k=SK)).then_inc(row_loaded, 16)
                    sp.dma_start(x_in[:, :, :], x.rearrange("(b p) f -> p b f", p=P)).then_inc(x_loaded, 16)
                    sp.wait_ge(ext_ready, 1)
                    for k in range(2):
                        sp.dma_start(ext_tab[k:k + 1, :].rearrange("o (p k) -> p (o k)", k=SK),
                                     tile_ext[:, k, :]).then_inc(ext_saved, 16)
                    sp.wait_ge(ext_saved, 32)
                    sp.dma_start(ext_bc[:, :, :], ext_tab.unsqueeze(0).to_broadcast([NB, 2, T])).then_inc(ext_loaded, 16)

                @block.scalar
                def _(act):
                    act.wait_ge(zero_ready, 1)
                    for j in range(TABLES):
                        act.dma_start(node_view(sum_tab[j]), zero_rows[:, :, :]).then_inc(zeroed, 16)
                        act.dma_start(sum_tab[j][NP:NP + P, :], zero_rows[:, 0, :]).then_inc(zeroed, 16)
                    act.wait_ge(zeroed, 32 * TABLES)

                @block.gpsimd
                def _(pool):
                    count = [0]

                    def link(ins):
                        count[0] += 1
                        ins.then_inc(pool_chain, 1)
                        pool.wait_ge(pool_chain, count[0])

                    pool.memset(zero_rows[:, :, :], 0.0).then_inc(zero_ready, 1)
                    pool.iota(iota_row[:, :], [[1, P]], base=0, channel_multiplier=0,
                              allow_small_or_imprecise_dtypes=True)
                    pool.iota(iota_b[:, :], [[1, P]], base=0, channel_multiplier=0,
                              allow_small_or_imprecise_dtypes=True)
                    pool.iota(node_id[:, :], [[P, NB]], base=0, channel_multiplier=1,
                              allow_small_or_imprecise_dtypes=True)
                    pool.iota(block_base[:, :], [[P, NB]], base=0, channel_multiplier=0,
                              allow_small_or_imprecise_dtypes=True)
                    pool.iota(trash[:, :], [[0, 1]], base=NP, channel_multiplier=1,
                              allow_small_or_imprecise_dtypes=True)
                    pool.iota(tile_up[:, :], [[1, T]], base=1, channel_multiplier=0,
                              allow_small_or_imprecise_dtypes=True)
                    pool.iota(bound[:, :], [[P, 2]], base=0, channel_multiplier=P,
                              allow_small_or_imprecise_dtypes=True)
                    pool.memset(dst_cnt[:, :], 0.0)
                    pool.memset(half[:, :], -0.5)
                    for m in (ident_f, below, above):
                        link(pool.memset(m[:, :], 0.0))
                    link(pool.affine_select(ident_f[:, :], ident_f[:, :], [[-1, P]], ALU.not_equal, 1.0,
                                            base=0, channel_multiplier=1))
                    link(pool.affine_select(below[:, :], below[:, :], [[1, P]], ALU.is_ge, 1.0,
                                            base=0, channel_multiplier=-1))
                    link(pool.affine_select(above[:, :], above[:, :], [[-1, P]], ALU.is_ge, 1.0,
                                            base=0, channel_multiplier=1))
                    pool.tensor_copy(ident_b[:, :], ident_f[:, :]).then_inc(const_ready, 1)
                    pool.wait_ge(pow_ask, 1)
                    pool.tensor_tensor(stat[:, :], stat[:, :], half[:, :], ALU.pow).then_inc(pow_done, 1)
                    pool.wait_ge(pow_ask, 2)
                    pool.tensor_tensor(deg_is[:, :], deg_is[:, :], half[:, :], ALU.pow).then_inc(pow_done, 1)

                @block.tensor
                def _(pe):
                    def count_chunk(k, wait):
                        pe.wait_ge(hot_ready, wait)
                        for c in range(HC):
                            last = pe.matmul(hist[:, :], hot_lo[k][:, c, :], hot_hi[k][:, c, :],
                                             start=False, stop=False, skip_group_check=True)
                        last.then_inc(hot_used, 1)

                    pe.wait_ge(const_ready, 1)
                    pe.wait_ge(hot_zero, 1)
                    pe.matmul(hist[:, :], hot_lo[0][:, 0, :], hot_hi[0][:, 0, :], start=True, stop=False,
                              skip_group_check=True).then_inc(hot_used, 2)
                    chunks = T // HC
                    with pe.Fori(0, chunks // 2) as r:
                        count_chunk(0, r * 2 + 1)
                        count_chunk(1, r * 2 + 2)
                    if chunks % 2:
                        count_chunk(0, chunks)
                    pe.wait_ge(runs_ready, 1)
                    pe.transpose(rows_ps[0:1, 0:NB], run[:, 0:1], ident_f[0:NB, 0:NB])
                    pe.transpose(rows_ps[0:1, NB:2 * NB], run[:, 1:2], ident_f[0:NB, 0:NB])
                    pe.matmul(rows_ps[0:1, 2 * NB:3 * NB], run[:, 1:2], above[0:NB, 0:NB],
                              start=True, stop=True).then_inc(rows_ready, 1)

                @block.vector
                def _(dve):
                    count = [0]

                    def link(ins):
                        count[0] += 1
                        ins.then_inc(chain, 1)
                        dve.wait_ge(chain, count[0])

                    for k in range(2):
                        dve.memset(hot_lo[k][:, :, :], 0.0)
                    dve.memset(hot_hi[1][:, :, :], 0.0)
                    dve.memset(hot_hi[0][:, :, :], 0.0).then_inc(hot_zero, 1)
                    dve.wait_ge(loaded, 32)
                    link(dve.tensor_copy(src_f[:, :], src_i[:, :]))
                    link(dve.tensor_copy(dst_f[:, :], dst_i[:, :]))
                    link(dve.tensor_scalar(dst_i[:, :], src_i[:, :], 7, None, ALU.logical_shift_right))
                    link(dve.tensor_copy(hi_b[:, :], dst_i[:, :]))
                    link(dve.tensor_scalar(dst_i[:, :], src_i[:, :], P - 1, None, ALU.bitwise_and))
                    link(dve.tensor_copy(lo_b[:, :], dst_i[:, :]))

                    dve.wait_ge(row_loaded, 16)
                    dve.tensor_reduce(tile_ext[:, 0, :], row_view[:, :, :], AX.X, ALU.min)
                    dve.tensor_reduce(tile_ext[:, 1, :], row_view[:, :, :], AX.X, ALU.max).then_inc(ext_ready, 1)

                    def hot_chunk(k, cols, wait):
                        dve.wait_ge(hot_used, wait)
                        dve.tensor_tensor(hot_lo[k][:, :, :], iota_b[:, :].unsqueeze(1).to_broadcast([P, HC, P]),
                                          lo_b[:, cols].unsqueeze(2).to_broadcast([P, HC, P]), ALU.is_equal)
                        dve.tensor_tensor(hot_hi[k][:, :, :], iota_b[:, 0:NB].unsqueeze(1).to_broadcast([P, HC, NB]),
                                          hi_b[:, cols].unsqueeze(2).to_broadcast([P, HC, NB]),
                                          ALU.is_equal).then_inc(hot_ready, 1)

                    dve.wait_ge(const_ready, 1)
                    chunks = T // HC
                    with dve.Fori(0, chunks // 2) as r:
                        hot_chunk(0, bass.ds(r * 2 * HC, HC), r * 2 + 1)
                        hot_chunk(1, bass.ds(r * 2 * HC + HC, HC), r * 2 + 2)
                    if chunks % 2:
                        hot_chunk(0, slice((chunks - 1) * HC, chunks * HC), chunks)

                    dve.wait_ge(ext_loaded, 16)
                    link(dve.scalar_tensor_tensor(ext_bc[:, 0, :], ext_bc[:, 0, :], bound[:, 1:2], tile_up[:, :],
                                                  ALU.is_lt, ALU.mult))
                    link(dve.tensor_reduce(run[:, 1:2], ext_bc[:, 0, :], AX.X, ALU.max))
                    link(dve.tensor_scalar(tile_up[:, :], tile_up[:, :], -1.0, float(T + 1), ALU.mult, ALU.add))
                    link(dve.scalar_tensor_tensor(ext_bc[:, 1, :], ext_bc[:, 1, :], bound[:, 0:1], tile_up[:, :],
                                                  ALU.is_ge, ALU.mult))
                    link(dve.tensor_reduce(run[:, 0:1], ext_bc[:, 1, :], AX.X, ALU.max))
                    link(dve.tensor_scalar(run[:, 0:1], run[:, 0:1], -1.0, float(T), ALU.mult, ALU.add))
                    link(dve.tensor_tensor(run[:, 1:2], run[:, 1:2], run[:, 0:1], ALU.subtract))
                    link(dve.tensor_scalar(run_i[:, :], run[:, 1:2], 1.0, float(GROUP - 1), ALU.max, ALU.add))
                    link(dve.tensor_scalar(run_i[:, :], run_i[:, :], GROUP.bit_length() - 1, None,
                                           ALU.logical_shift_right))
                    dve.tensor_copy(run[:, 1:2], run_i[:, :]).then_inc(runs_ready, 1)
                    dve.wait_ge(rows_ready, 1)
                    link(dve.tensor_copy(row[0:1, 0:3, :].rearrange("o a b -> o (a b)"), rows_ps[0:1, :]))
                    link(dve.tensor_tensor(row_i[:, 0:1], row[:, 1, NB - 1:NB], row[:, 2, NB - 1:NB], ALU.add))
                    link(dve.tensor_scalar(row_i[:, 1:2], row_i[:, 0:1], 1, None, ALU.bitwise_and))
                    link(dve.tensor_tensor(row[:, 1, NB - 1:NB], row[:, 1, NB - 1:NB], row_i[:, 1:2], ALU.add))
                    link(dve.tensor_scalar(row_i[:, 0:1], row_i[:, 0:1], 1.0, None, ALU.add))
                    link(dve.tensor_scalar(sched[:, 3 * NB:], row_i[:, 0:1], 1, None, ALU.logical_shift_right))
                    link(dve.tensor_scalar(row[:, 3, :], row[:, 1, :], -float(GROUP), float(TP), ALU.mult, ALU.add))
                    link(dve.tensor_tensor(sched[:, 0:NB], row[:, 0, :], row[:, 3, :], ALU.min))
                    link(dve.tensor_copy(sched[:, NB:3 * NB], row[0:1, 1:3, :].rearrange("o a b -> o (a b)")))

                    dve.wait_ge(x_loaded, 16)
                    dve.wait_ge(zeroed, 32 * TABLES)

                    def power(step):
                        def go():
                            dve.sem_inc(pow_ask, 1)
                            dve.wait_ge(pow_done, step)
                        return go

                    layer_norm(dve, link, power(1), x_in[:, :, :], scratch[:, :, :])
                    dve.wait_ge(hot_used, chunks + 2)
                    link(dve.tensor_scalar(deg_is[:, :], hist[:, :], 1.0, None, ALU.max))
                    power(2)()
                    link(dve.scalar_tensor_tensor(deg_is[:, :], hist[:, :], 0.0, deg_is[:, :], ALU.is_gt, ALU.mult))
                    link(dve.tensor_tensor(scratch[:, :, :], act_in[:, :, :],
                                           deg_is[:, :].unsqueeze(2).to_broadcast([P, NB, F]), ALU.mult))
                    for k in range(PLANES):
                        link(dve.tensor_copy(g_planes[:, :, k, :], scratch[:, :, :]))
                        if k < PLANES - 1:
                            link(dve.tensor_tensor(scratch[:, :, :], scratch[:, :, :], g_planes[:, :, k, :],
                                                   ALU.subtract))

            with ExitStack() as ctx:
                s4 = sb("s4", [P, GROUP], F32, ctx)
                d4 = sb("d4", [P, GROUP], F32, ctx)
                hot_t = sb("hot_t", [P, W], BF16, ctx)
                same = sb("same", [P, GROUP, P], F32, ctx)
                junk = sb("junk", [P, GROUP, P], F32, ctx)
                dup = sb("dup", [P, GROUP], F32, ctx)
                moved = sb("moved", [P, GROUP], F32, ctx)
                in_group = sb("in_group", [P, 1], F32, ctx)
                rows = sb("rows", [P, GROUP, F], F32, ctx)
                vals = sb("vals", [P, 2, GROUP, F], F32, ctx)
                idx = sb("idx", [P, 2, GROUP], I32, ctx)
                src_t = ps("src_t", [P, W], F32, ctx)
                dst_t = ps("dst_t", [P, W], F32, ctx)
                rows_p = ps("rows_p", [P, GROUP, F], F32, ctx)
                comb_p = ps("comb_p", [P, GROUP, F], F32, ctx)

                cols_ready = sem("cols_ready", ctx)
                cols_used = sem("cols_used", ctx)
                ids_ready = sem("ids_ready", ctx)
                hot_ready = sem("hot_t_ready", ctx)
                same_ready = sem("same_ready", ctx)
                rows_made = sem("rows_made", ctx)
                rows_ready = sem("rows_kept", ctx)
                comb_made = sem("comb_made", ctx)
                vals_ready = sem("vals_ready", ctx)
                idx_ready = sem("idx_ready", ctx)
                slot_free = sem("slot_free", ctx)
                turns = sem("turns", ctx)
                scattered = [sem(f"scattered{j}", ctx) for j in range(TABLES)]
                steps = sem("steps", ctx)
                prime = sem("prime", ctx)
                block = ctx.enter_context(nc.Block())

                @block.scalar
                def _(act):
                    with act.Fori(0, NB) as b:
                        first, groups, before = load_block(act, b)
                        with act.Fori(0, groups) as i:
                            q = act.snap(before + i)
                            t = tile_of(act, first, i)
                            act.wait_ge(cols_used, q + 1)
                            act.copy(s4[:, :], src_f[:, bass.ds(t, GROUP)])
                            act.copy(d4[:, :], dst_f[:, bass.ds(t, GROUP)]).then_inc(cols_ready, 1)
                            act.wait_ge(rows_made, q + 1)
                            act.copy(rows[:, :, :], rows_p[:, :, :]).then_inc(rows_ready, 1)
                            act.wait_ge(comb_made, q + 1)
                            act.wait_ge(slot_free, q + 1)
                            act.copy(vals[:, bass.ds(q % 2, 1), :, :].rearrange("p o g f -> p (o g) f"),
                                     comb_p[:, :, :]).then_inc(vals_ready, 1)

                @block.tensor
                def _(pe):
                    with pe.Fori(0, NB) as b:
                        first, groups, before = load_block(pe, b)
                        with pe.Fori(0, groups) as i:
                            q = pe.snap(before + i)
                            pe.wait_ge(cols_ready, q + 1)
                            for j in range(GROUP):
                                pe.transpose(dst_t[:, j * P:(j + 1) * P], d4[:, j:j + 1].to_broadcast([P, P]), ident_f[:, :])
                            for j in range(GROUP):
                                last = pe.transpose(src_t[:, j * P:(j + 1) * P], s4[:, j:j + 1].to_broadcast([P, P]),
                                                    ident_f[:, :])
                            last.then_inc(ids_ready, 1)
                            pe.wait_ge(hot_ready, q + 1)
                            for j in range(GROUP):
                                for k in range(PLANES):
                                    last = pe.matmul(rows_p[:, j, :], hot_t[:, j * P:(j + 1) * P],
                                                     g_planes[:, bass.ds(b, 1), k, :].rearrange("p o f -> p (o f)"),
                                                     start=(k == 0), stop=(k == PLANES - 1))
                            last.then_inc(rows_made, 1)
                            pe.wait_ge(same_ready, q + 1)
                            pe.wait_ge(rows_ready, q + 1)
                            for j in range(GROUP):
                                last = pe.matmul(comb_p[:, j, :], same[:, j, :], rows[:, j, :], start=True, stop=True)
                            last.then_inc(comb_made, 1)

                STEPS = 3

                @block.vector
                def _(dve):
                    dve.memset(junk[:, :, :], 0.0)
                    dve.memset(vals[:, :, :, :], 0.0)
                    dve.tensor_copy(idx[:, :, :].rearrange("p a g -> p (a g)"),
                                    trash[:, 0:1].to_broadcast([P, 2 * GROUP])).then_inc(prime, 1)
                    dve.sem_inc(cols_used, 1)
                    with dve.Fori(0, NB) as b:
                        first, groups, before = load_block(dve, b)
                        with dve.Fori(0, groups) as i:
                            q = dve.snap(before + i)
                            s = dve.snap(q * STEPS)
                            dve.wait_ge(ids_ready, q + 1)
                            dve.tensor_scalar(hot_t[:, :], dst_t[:, :], node_id[:, bass.ds(b, 1)], None,
                                              ALU.is_equal).then_inc(hot_ready, 1)
                            for j in range(GROUP):
                                last = dve.tensor_scalar(same[:, j, :], src_t[:, j * P:(j + 1) * P], s4[:, j:j + 1], None,
                                                         ALU.is_equal)
                            last.then_inc(same_ready, 1)
                            dve.wait_ge(same_ready, q + 1)
                            dve.tensor_reduce(in_group[:, :], hot_t[:, :], AX.X, ALU.add).then_inc(steps, 1)
                            for j in range(GROUP):
                                last = dve.tensor_tensor_reduce(junk[:, j, :], same[:, j, :], below[:, :], 1.0, 0.0, ALU.mult,
                                                                ALU.max, dup[:, j:j + 1])
                            last.then_inc(steps, 1)
                            dve.wait_ge(steps, s + 2)
                            dve.scalar_tensor_tensor(moved[:, :], s4[:, :], trash[:, 0:1], dup[:, :], ALU.subtract,
                                                     ALU.mult).then_inc(steps, 1)
                            dve.wait_ge(steps, s + 3)
                            dve.wait_ge(slot_free, q + 1)
                            dve.tensor_tensor(idx[:, bass.ds(q % 2, 1), :].rearrange("p o g -> p (o g)"),
                                              s4[:, :], moved[:, :], ALU.subtract).then_inc(idx_ready, 1)
                            dve.wait_ge(cols_used, q + 1)
                            dve.tensor_tensor(dst_cnt[:, bass.ds(b, 1)], dst_cnt[:, bass.ds(b, 1)], in_group[:, :],
                                              ALU.add).then_inc(cols_used, 1)

                @block.gpsimd
                def _(pool):
                    def scatter(k, j):
                        pool.indirect_dma_start(sum_tab[j], bass.IndirectOffsetOnAxis(idx[:, k, j:j + 1], 0),
                                                vals[:, k, j, :], None, compute_op=ALU.add).then_inc(scattered[j], 16)

                    pool.wait_ge(prime, 1)
                    for j in range(TABLES):
                        scatter(0, j)
                    for j in range(TABLES):
                        pool.wait_ge(scattered[j], 16)
                    pool.sem_inc(slot_free, 1)
                    pairs = pool.value_load(sched[0:1, 3 * NB:3 * NB + 1], min_val=1, max_val=NB * MOST)
                    with pool.Fori(0, pairs) as r:
                        for k in range(2):
                            q = pool.snap(r * 2 + k)
                            pool.wait_ge(vals_ready, q + 1)
                            pool.wait_ge(idx_ready, q + 1)
                            for j in range(TABLES):
                                pool.wait_ge(scattered[j], q * 16 + 16)
                                pool.sem_inc(turns, 1)
                                if j == TABLES - 1:
                                    pool.sem_inc(slot_free, 1)
                                scatter(k, j)
                    for j in range(TABLES):
                        pool.wait_ge(scattered[j], pairs * 32 + 16)

        with ExitStack() as q_life:
            q_planes = sb("q_planes", [P, NB, PLANES, H], BF16, q_life)
            nb2 = sb("nb2", [P, H], F32, q_life)
            b1_col = sb("b1_col", [H, 1], F32, q_life)
            w1c_sb = sb("w1c_sb", [P, H], F32, q_life)
            w2_sb = sb("w2_sb", [H, H], F32, q_life)
            w3_sb = sb("w3_sb", [H, F], F32, q_life)
            c_bc = sb("c_bc", [P, F], F32, q_life)
            with ExitStack() as ctx:
                NT = TABLES
                flat = q_planes[:, :, :, :].rearrange("p b k h -> p (b k h)").bitcast(F32)
                sums = [flat[:, j * NB * F:(j + 1) * NB * F].rearrange("p (b f) -> p b f", b=NB) for j in range(NT)]
                w0_sb = sb("w0_sb", [F, F], F32, ctx)
                w1_sb = sb("w1_sb", [F, 2 * H], F32, ctx)
                b0_bc = sb("b0_bc", [P, F], F32, ctx)
                b3_bc = sb("b3_bc", [P, F], F32, ctx)
                b2_col = sb("b2_col", [H, 1], F32, ctx)
                blk = sb("blk", [P, CB, F], F32, ctx)
                blk_t = sb("blk_t", [F, CB, P], F32, ctx)
                y = sb("y", [P, CB, F], F32, ctx)
                rest = sb("rest", [P, CB, 2 * H], F32, ctx)
                p_out = sb("p_out", [P, CB, PLANES, H], BF16, ctx)
                t_ps = ps("t_ps", [F, 8, P], F32, ctx)
                y_ps = ps("y_ps", [P, CB, F], F32, ctx)
                pq_ps = ps("pq_ps", [P, 8, 2 * H], F32, ctx)
                c_ps = ps("c_ps", [P, F], F32, ctx)

                sum_loaded = [sem(f"sum_loaded{j}", ctx) for j in range(NT)]
                summed = sem("summed", ctx)
                w_loaded = sem("w_loaded", ctx)
                chain = sem("chain_c", ctx)
                blk_ready = sem("blk_ready", ctx)
                t_made = sem("t_made", ctx)
                t_ready = sem("t_ready", ctx)
                y_made = sem("y_made", ctx)
                c_made = sem("c_made", ctx)
                plane_ready = sem("plane_ready", ctx)
                p_stored = sem("p_stored", ctx)
                pow_ask = sem("pow_ask_c", ctx)
                pow_done = sem("pow_done_c", ctx)
                rest_ready = sem("rest_ready", ctx)
                w1c_zero = sem("w1c_zero", ctx)
                y_ready = sem("y_ready", ctx)
                p_zero = sem("p_zero", ctx)
                turns = sem("turns_c", ctx)
                sp_turns = sem("sp_turns", ctx)
                x1_ready = sem("x1_ready", ctx)
                block = ctx.enter_context(nc.Block())

                @block.sync
                def _(sp):
                    for j in range(NT):
                        sp.dma_start(sums[j], node_view(sum_tab[j])).then_inc(sum_loaded[j], 16)
                    sp.dma_start(w0_sb[:, :], w0_t).then_inc(w_loaded, 16)
                    sp.dma_start(w1_sb[:, :], w1ab).then_inc(w_loaded, 16)
                    sp.dma_start(w2_sb[:, :], w2).then_inc(w_loaded, 16)
                    sp.dma_start(w3_sb[:, :], w3).then_inc(w_loaded, 16)
                    sp.dma_start(b0_bc[:, :], b0.to_broadcast([P, F])).then_inc(w_loaded, 16)
                    sp.dma_start(b3_bc[:, :], b3.to_broadcast([P, F])).then_inc(w_loaded, 16)
                    sp.dma_start(nb2[:, :], b2.to_broadcast([P, H])).then_inc(w_loaded, 16)
                    sp.dma_start(b1_col[:, :], b1).then_inc(w_loaded, 16)
                    sp.dma_start(b2_col[:, :], b2.rearrange("o h -> h o")).then_inc(w_loaded, 16)
                    sp.wait_ge(w1c_zero, 1)
                    sp.dma_start(w1c_sb[0:EF, :], w1c).then_inc(w_loaded, 16)
                    sp.wait_ge(p_zero, 1)
                    sp.dma_start(p_tab[0:P, :], p_out[:, 0, :, :].rearrange("p k h -> p (k h)")).then_inc(p_stored, 16)
                    sp.wait_ge(p_stored, 16)
                    with sp.Fori(0, NK) as k:
                        sp.wait_ge(plane_ready, (k + 1) * 6)
                        sp.dma_start(p_tab.rearrange("(b p) f -> p b f", p=P)[:, bass.ds(k * CB, CB), :],
                                     p_out[:, :, :, :].rearrange("p b k h -> p b (k h)")).then_inc(p_stored, 16)
                        sp.wait_ge(p_stored, (k + 2) * 16)
                        sp.sem_inc(sp_turns, 1)

                W_LOADS = 10

                def power(dve):
                    def go():
                        dve.sem_inc(pow_ask, 1)
                        dve.wait_ge(pow_done, 1)
                    return go

                @block.gpsimd
                def _(pool):
                    pool.memset(w1c_sb[:, :], 0.0).then_inc(w1c_zero, 1)
                    pool.memset(p_out[:, 0, :, :], 0.0).then_inc(p_zero, 1)
                    pool.wait_ge(pow_ask, 1)
                    pool.tensor_tensor(stat[:, :], stat[:, :], half[:, :], ALU.pow).then_inc(pow_done, 1)

                @block.tensor
                def _(pe):
                    pe.wait_ge(w_loaded, 16 * W_LOADS)
                    pe.matmul(c_ps[:, :], b2_col[:, 0:1].to_broadcast([H, P]), w3_sb[:, :], start=True,
                              stop=True).then_inc(c_made, 1)

                    def turn(n):
                        pe.wait_ge(blk_ready, n + 1)
                        pe.sem_inc(turns, 1)
                        for c in range(CB):
                            last = pe.transpose(t_ps[:, c, :], blk[:, c, :], ident_f[:, :])
                        last.then_inc(t_made, 1)
                        pe.wait_ge(t_ready, n + 1)

                    with pe.Fori(0, NK) as k:
                        turn(k)
                        for c in range(CB):
                            last = pe.matmul(y_ps[:, c, :], blk_t[:, c, :], w0_sb[:, :], start=True, stop=True)
                        last.then_inc(y_made, 1)
                    with pe.Fori(0, NK) as k:
                        turn(k + NK)
                        for c in range(CB):
                            last = pe.matmul(pq_ps[:, c, :], blk_t[:, c, :], w1_sb[:, :], start=True, stop=True)
                        last.then_inc(y_made, 1)

                @block.scalar
                def _(act):
                    with act.Fori(0, NK) as k:
                        act.wait_ge(t_made, k + 1)
                        act.copy(blk_t[:, :, :], t_ps[:, 0:CB, :]).then_inc(t_ready, 1)
                    with act.Fori(0, NK) as k:
                        act.wait_ge(t_made, k + (NK + 1))
                        act.copy(blk_t[:, :, :], t_ps[:, 0:CB, :]).then_inc(t_ready, 1)
                        act.wait_ge(y_made, k + (NK + 1))
                        act.wait_ge(p_stored, k * 16 + 16)
                        for m in range(PLANES):
                            if m:
                                act.wait_ge(rest_ready, k * 2 + m)
                            v = pq_ps[:, 0:CB, :] if m == 0 else rest[:, :, :]
                            act.copy(p_out[:, :, m, :], v[:, :, 0:H]).then_inc(plane_ready, 1)
                            act.copy(q_planes[:, bass.ds(k * CB, CB), m, :], v[:, :, H:2 * H]).then_inc(plane_ready, 1)

                @block.vector
                def _(dve):
                    count = [0]

                    def link(ins):
                        count[0] += 1
                        ins.then_inc(chain, 1)
                        dve.wait_ge(chain, count[0])

                    dve.wait_ge(sum_loaded[0], 16)
                    for j in range(1, NT):
                        dve.wait_ge(sum_loaded[j], 16)
                        dve.tensor_tensor(sums[0], sums[0], sums[j], ALU.add).then_inc(summed, 1)
                        dve.wait_ge(summed, j)
                    dve.wait_ge(w_loaded, 16 * W_LOADS)
                    link(dve.tensor_scalar(nb2[:, :], nb2[:, :], -1.0, None, ALU.mult))
                    dve.wait_ge(c_made, 1)
                    link(dve.tensor_tensor(c_bc[:, :], c_ps[:, :], b3_bc[:, :], ALU.add))
                    with dve.Fori(0, NK) as k:
                        blocks = bass.ds(k * CB, CB)
                        dve.tensor_tensor(blk[:, :, :], sums[0][:, blocks, :],
                                          deg_is[:, blocks].unsqueeze(2).to_broadcast([P, CB, F]),
                                          ALU.mult).then_inc(blk_ready, 1)
                        dve.wait_ge(y_made, k + 1)
                        dve.tensor_tensor(y[:, :, :], y_ps[:, :, :], b0_bc[:, :].unsqueeze(1).to_broadcast([P, CB, F]),
                                          ALU.add).then_inc(y_ready, 1)
                        dve.wait_ge(y_ready, k + 1)
                        dve.scalar_tensor_tensor(x1[:, blocks, :], y[:, :, :], 0.0, x1[:, blocks, :], ALU.max,
                                                 ALU.add).then_inc(x1_ready, 1)
                    dve.wait_ge(x1_ready, NK)
                    layer_norm(dve, link, power(dve), x1[:, :, :], sums[0])
                    with dve.Fori(0, NK) as k:
                        blocks = bass.ds(k * CB, CB)
                        dve.tensor_copy(blk[:, :, :], act_in[:, blocks, :]).then_inc(blk_ready, 1)
                        for m in range(PLANES - 1):
                            dve.wait_ge(plane_ready, k * 6 + 2 * m + 2)
                            v = pq_ps[:, 0:CB, :] if m == 0 else rest[:, :, :]
                            for w, pl in ((0, p_out[:, :, m, :]), (1, q_planes[:, blocks, m, :])):
                                last = dve.tensor_tensor(rest[:, :, w * H:(w + 1) * H], v[:, :, w * H:(w + 1) * H], pl,
                                                         ALU.subtract)
                            last.then_inc(rest_ready, 1)

            upd = sb("upd", [P, NB, F], F32, q_life)
            with ExitStack() as ctx:
                d4 = sb("d4_d", [P, GROUP], F32, ctx)
                idx = sb("idx_d", [P, 2, GROUP], I32, ctx)
                p_got = sb("p_got", [P, 2, GROUP, PLANES * H], BF16, ctx)
                ef = sb("ef", [P, 2, W], F32, ctx)
                row_id = sb("row_id", [P, P], F32, ctx)
                hot = sb("hot", [P, 2, GROUP, P], F32, ctx)
                hot_t = sb("hot_t_d", [P, W], BF16, ctx)
                h1 = [sb(f"h1_{k}", [H, W // 2], F32, ctx) for k in range(2)]
                h2 = [sb(f"h2_{k}", [P, 2, H], F32, ctx) for k in range(2)]
                seg = sb("seg", [H, P], F32, ctx)
                zero_w = sb("zero_w", [P, P], BF16, ctx)
                dst_t = ps("dst_t_d", [P, W], F32, ctx)
                z1 = [ps(f"z1_{k}", [H, 512], F32, ctx) for k in range(2)]
                z2 = [ps(f"z2_{k}", [P, 4, H], F32, ctx) for k in range(2)]
                seg_ps = ps("seg_ps", [H, P], F32, ctx)
                m_ps = ps("m_ps", [P, F], F32, ctx)

                ef_loaded = sem("ef_loaded", ctx)
                ef_zero = sem("ef_zero", ctx)
                ef_used = sem("ef_used", ctx)
                cols_ready = sem("cols_ready_d", ctx)
                ids_ready = sem("ids_ready_d", ctx)
                hot_ready = sem("hot_ready_d", ctx)
                hot_t_ready = sem("hot_t_ready_d", ctx)
                gathered = [sem(f"gathered{j}", ctx) for j in range(GROUP)]
                p_used = sem("p_used", ctx)
                turns = sem("turns_d", ctx)
                sp_turns = sem("sp_turns_d", ctx)
                z1_made = sem("z1_made", ctx)
                h1_ready = sem("h1_ready", ctx)
                z2_made = sem("z2_made", ctx)
                h2_ready = sem("h2_ready", ctx)
                seg_used = sem("seg_used", ctx)
                seg_made = sem("seg_made", ctx)
                seg_ready = sem("seg_ready", ctx)
                m_made = sem("m_made", ctx)
                id_ready = sem("id_ready", ctx)
                zero_w_ready = sem("zero_w_ready", ctx)
                primed = sem("primed", ctx)
                prime = sem("prime_d", ctx)
                block = ctx.enter_context(nc.Block())

                @block.sync
                def _(sp):
                    sp.wait_ge(ef_zero, 1)
                    sp.dma_start(ef[0:EF, 0, :], edge_t[:, 0:W]).then_inc(ef_loaded, 16)
                    with sp.Fori(0, NB) as b:
                        first, groups, before = load_block(sp, b)
                        with sp.Fori(0, groups) as i:
                            q = sp.snap(before + i)
                            par = sp.snap(q % 2)
                            edge = sp.snap(tile_of(sp, first, i) * P)
                            sp.wait_ge(ef_loaded, q * 16 + 16)
                            sp.sem_inc(sp_turns, 1)
                            sp.wait_ge(ef_used, q + 1)
                            sp.dma_start(ef[0:EF, bass.ds(par, 1), :].rearrange("p o w -> p (o w)"),
                                         edge_t[:, bass.ds(edge, W)]).then_inc(ef_loaded, 16)

                @block.gpsimd
                def _(pool):
                    def gather(k, j):
                        pool.indirect_dma_start(p_got[:, k, j, :], None, p_tab,
                                                bass.IndirectOffsetOnAxis(idx[:, k, j:j + 1], 0)
                                                ).then_inc(gathered[j], 16)

                    pool.memset(ef[:, :, :], 0.0).then_inc(ef_zero, 1)
                    pool.wait_ge(prime, 1)
                    for n in range(2):
                        for j in range(GROUP):
                            gather(n, j)
                        for j in range(GROUP):
                            pool.wait_ge(gathered[j], 16 * n + 16)
                    pool.sem_inc(primed, 1)
                    pairs = pool.value_load(sched[0:1, 3 * NB:3 * NB + 1], min_val=1, max_val=NB * MOST)
                    with pool.Fori(0, pairs) as r:
                        for k in range(2):
                            q = pool.snap(r * 2 + k)
                            pool.wait_ge(cols_ready, q + 1)
                            pool.wait_ge(p_used, q + 1)
                            for j in range(GROUP):
                                pool.wait_ge(gathered[j], q * 16 + 32)
                                pool.sem_inc(turns, 1)
                                gather(k, j)
                    for j in range(GROUP):
                        pool.wait_ge(gathered[j], pairs * 32 + 32)

                @block.scalar
                def _(act):
                    act.copy(idx[:, 0, :], src_i[:, 0:GROUP])
                    act.copy(idx[:, 1, :], src_i[:, 0:GROUP]).then_inc(prime, 1)
                    act.wait_ge(primed, 1)
                    with act.Fori(0, NB) as b:
                        first, groups, before = load_block(act, b)
                        with act.Fori(0, groups) as i:
                            q = act.snap(before + i)
                            t = tile_of(act, first, i)
                            act.copy(d4[:, :], dst_f[:, bass.ds(t, GROUP)])
                            for j in range(GROUP):
                                act.wait_ge(gathered[j], q * 16 + 16)
                            act.copy(idx[:, bass.ds(q % 2, 1), :].rearrange("p o g -> p (o g)"),
                                     src_i[:, bass.ds(t, GROUP)]).then_inc(cols_ready, 1)
                            for k in range(2):
                                act.wait_ge(z1_made, q * 2 + (k + 1))
                                act.activation(h1[k][:, :], z1[k][:, 0:W // 2], ACT.Relu,
                                               bias=b1_col[:, 0:1]).then_inc(h1_ready, 1)
                        act.wait_ge(seg_made, b + 1)
                        act.copy(seg[:, :], seg_ps[:, :]).then_inc(seg_ready, 1)

                @block.tensor
                def _(pe):
                    pe.sem_inc(ef_used, 2)
                    pe.sem_inc(p_used, 2)
                    pe.sem_inc(seg_used, 2)
                    pe.wait_ge(zero_w_ready, 1)
                    with pe.Fori(0, NB) as b:
                        first, groups, before = load_block(pe, b)
                        pe.matmul(seg_ps[:, :], zero_w[:, :], zero_w[:, :], start=True, stop=False,
                                  skip_group_check=True)
                        with pe.Fori(0, groups) as i:
                            q = pe.snap(before + i)
                            par = pe.snap(q % 2)
                            pe.wait_ge(cols_ready, q + 1)
                            for j in range(GROUP):
                                last = pe.transpose(dst_t[:, j * P:(j + 1) * P], d4[:, j:j + 1].to_broadcast([P, P]),
                                                    ident_f[:, :])
                            last.then_inc(ids_ready, 1)
                            pe.wait_ge(ef_loaded, q * 16 + 32)
                            for k in range(2):
                                last = pe.matmul(z1[k][:, 0:W // 2], w1c_sb[:, :],
                                                 ef[:, bass.ds(par, 1), k * W // 2:(k + 1) * W // 2].rearrange("p o w -> p (o w)"),
                                                 start=True, stop=False)
                            last.then_inc(ef_used, 1)
                            for k in range(2):
                                for j in range(2):
                                    pe.wait_ge(gathered[2 * k + j], q * 16 + 48)
                                    for m in range(PLANES):
                                        last = pe.matmul(z1[k][:, j * P:(j + 1) * P],
                                                         p_got[:, bass.ds(par, 1), 2 * k + j, m * H:(m + 1) * H]
                                                         .rearrange("p o h -> p (o h)"),
                                                         ident_b[:, :], start=False, stop=False)
                                if k == 1:
                                    last.then_inc(p_used, 1)
                                else:
                                    pe.wait_ge(hot_t_ready, q + 1)
                                for m in range(PLANES):
                                    last = pe.matmul(z1[k][:, 0:W // 2],
                                                     q_planes[:, bass.ds(b, 1), m, :].rearrange("p o h -> p (o h)"),
                                                     hot_t[:, k * W // 2:(k + 1) * W // 2], start=False,
                                                     stop=(m == PLANES - 1))
                                last.then_inc(z1_made, 1)
                            for k in range(2):
                                pe.wait_ge(h1_ready, q * 2 + (k + 1))
                                for j in range(2):
                                    last = pe.matmul(z2[k][:, j, :], h1[k][:, j * P:(j + 1) * P], w2_sb[:, :],
                                                     start=True, stop=True)
                                last.then_inc(z2_made, 1)
                            for k in range(2):
                                pe.wait_ge(h2_ready, q * 2 + (k + 1))
                                if k == 0:
                                    pe.wait_ge(hot_ready, q + 1)
                                for j in range(2):
                                    last = pe.matmul(seg_ps[:, :], h2[k][:, j, :],
                                                     hot[:, bass.ds(par, 1), 2 * k + j, :].rearrange("p o n -> p (o n)"),
                                                     start=False, stop=False, skip_group_check=True)
                            last.then_inc(seg_used, 1)
                        pe.matmul(seg_ps[:, :], zero_w[:, :], zero_w[:, :], start=False, stop=True,
                                  skip_group_check=True).then_inc(seg_made, 1)
                        pe.wait_ge(seg_ready, b + 1)
                        pe.matmul(m_ps[:, :], seg[:, :], w3_sb[:, :], start=True, stop=True).then_inc(m_made, 1)

                @block.vector
                def _(dve):
                    dve.memset(zero_w[:, :], 0.0).then_inc(zero_w_ready, 1)
                    with dve.Fori(0, NB) as b:
                        first, groups, before = load_block(dve, b)
                        dve.tensor_scalar(row_id[:, :], iota_row[:, :], block_base[:, bass.ds(b, 1)], None,
                                          ALU.add).then_inc(id_ready, 1)
                        with dve.Fori(0, groups) as i:
                            q = dve.snap(before + i)
                            dve.wait_ge(cols_ready, q + 1)
                            dve.wait_ge(seg_used, q + 1)
                            dve.wait_ge(id_ready, b + 1)
                            dve.tensor_tensor(hot[:, bass.ds(q % 2, 1), :, :].rearrange("p o g n -> p (o g) n"),
                                              row_id[:, :].unsqueeze(1).to_broadcast([P, GROUP, P]),
                                              d4[:, :].unsqueeze(2).to_broadcast([P, GROUP, P]),
                                              ALU.is_equal).then_inc(hot_ready, 1)
                            dve.wait_ge(ids_ready, q + 1)
                            dve.tensor_scalar(hot_t[:, :], dst_t[:, :], node_id[:, bass.ds(b, 1)], None,
                                              ALU.is_equal).then_inc(hot_t_ready, 1)
                            for k in range(2):
                                dve.wait_ge(z2_made, q * 2 + (k + 1))
                                dve.tensor_tensor(h2[k][:, :, :], z2[k][:, 0:2, :],
                                                  nb2[:, :].unsqueeze(1).to_broadcast([P, 2, H]),
                                                  ALU.max).then_inc(h2_ready, 1)
                        dve.wait_ge(m_made, b + 1)
                        dve.tensor_copy(upd[:, bass.ds(b, 1), :].rearrange("p o f -> p (o f)"), m_ps[:, :])

            with ExitStack() as ctx:
                inv = sb("inv", [P, NB], F32, ctx)
                chain = sem("chain_e", ctx)
                final = sem("final", ctx)
                stored = sem("stored", ctx)
                block = ctx.enter_context(nc.Block())

                @block.vector
                def _(dve):
                    count = [0]

                    def link(ins):
                        count[0] += 1
                        ins.then_inc(chain, 1)
                        dve.wait_ge(chain, count[0])

                    full = [P, NB, F]
                    scratch = q_planes[:, :, :, :].rearrange("p b k h -> p (b k h)").bitcast(F32)[:, 0:NB * F]\
                        .rearrange("p (b f) -> p b f", b=NB)
                    link(dve.tensor_tensor(scratch, dst_cnt[:, :].unsqueeze(2).to_broadcast(full),
                                           c_bc[:, :].unsqueeze(1).to_broadcast(full), ALU.mult))
                    link(dve.tensor_tensor(upd[:, :, :], upd[:, :, :], scratch, ALU.add))
                    link(dve.tensor_scalar(inv[:, :], dst_cnt[:, :], 1.0, None, ALU.max))
                    link(dve.reciprocal(inv[:, :], inv[:, :]))
                    link(dve.tensor_tensor(upd[:, :, :], upd[:, :, :], inv[:, :].unsqueeze(2).to_broadcast(full),
                                           ALU.mult))
                    link(dve.tensor_tensor(upd[:, :, :], upd[:, :, :], act_in[:, :, :], ALU.add))
                    dve.tensor_tensor(upd[:, :, :], upd[:, :, :], x1[:, :, :], ALU.add).then_inc(final, 1)

                @block.sync
                def _(sp):
                    whole_blocks = N // P
                    sp.wait_ge(final, 1)
                    sp.dma_start(out[0:whole_blocks * P, :].rearrange("(b p) f -> p b f", p=P),
                                 upd[:, 0:whole_blocks, :]).then_inc(stored, 16)
                    if N % P:
                        sp.dma_start(out[whole_blocks * P:N, :], upd[0:N % P, whole_blocks, :]).then_inc(stored, 16)
                    sp.wait_ge(stored, 16 * (1 + (N % P > 0)))


def layout(x, src, dst, edge_attr_16, L0_gnn_W, L0_gnn_b, L1_gnn_W1, L1_gnn_b1, L1_gnn_W2, L1_gnn_b2, L1_gnn_W3,
           L1_gnn_b3):
    import numpy as np

    def a(v):
        return np.ascontiguousarray(v)

    n, f = x.shape
    e, ef = edge_attr_16.shape
    tiles = e // P
    padded = GROUP * (-(-tiles // GROUP) + 1)
    more = padded * P - e
    h = L1_gnn_W2.shape[0]
    src_p = np.concatenate([src, np.zeros(more, src.dtype)])
    dst_p = np.concatenate([dst, np.full(more, PAD_NODE, dst.dtype)])
    w1 = np.asarray(L1_gnn_W1)
    return {
        "x": a(np.concatenate([x, np.zeros((-n % P, f), x.dtype)])),
        "src_col": a(src_p.reshape(padded, P).T),
        "dst_col": a(dst_p.reshape(padded, P).T),
        "dst_row": a(np.asarray(dst).reshape(tiles, P)),
        "edge_t": a(np.concatenate([edge_attr_16, np.zeros((more, ef), edge_attr_16.dtype)]).T),
        "w0_t": a(np.asarray(L0_gnn_W).T),
        "b0": a(np.asarray(L0_gnn_b).reshape(1, f)),
        "w1ab": a(np.concatenate([w1[0:f], w1[f:2 * f]], axis=1)),
        "w1c": a(w1[2 * f:]),
        "b1": a(np.asarray(L1_gnn_b1).reshape(h, 1)),
        "w2": a(L1_gnn_W2),
        "b2": a(np.asarray(L1_gnn_b2).reshape(1, h)),
        "w3": a(L1_gnn_W3),
        "b3": a(np.asarray(L1_gnn_b3).reshape(1, f)),
    }


def kernel(**inputs):
    import numpy as np
    import concourse.bacc as bacc
    from concourse.bass_utils import run_bass_kernel_spmd

    inputs = {k: np.asarray(v) for k, v in inputs.items()}
    nc = bacc.Bacc("TRN2", target_bir_lowering=False, num_devices=1)
    arrays = layout(**inputs)
    args = [nc.dram_tensor(f"in_{k}", v.shape, mybir.dt.from_np(v.dtype), kind="ExternalInput").ap()
            for k, v in arrays.items()]
    out = nc.dram_tensor("out_0", inputs["x"].shape, F32, kind="ExternalOutput").ap()
    build_gnn(nc, *args, out)
    r = run_bass_kernel_spmd(nc, [{f"in_{k}": v for k, v in arrays.items()}], core_ids=[0])
    return r.results[0]["out_0"]
```

```python
from contextlib import ExitStack

import concourse.bass as bass
from concourse import mybir

P = 128
GROUP = 4
UNROLL = 4
TABLES = GROUP
PLANES = 3
PAD_NODE = 1 << 20
EPS = 1e-5

ALU = mybir.AluOpType
ACT = mybir.ActivationFunctionType
AX = mybir.AxisListType
F32 = mybir.dt.float32
BF16 = mybir.dt.bfloat16
I32 = mybir.dt.int32


def divisor(n, most):
    return max(d for d in range(1, most + 1) if n % d == 0)


def paced(eng, steps, body):
    for s in range(UNROLL):
        body(s, s)
    with eng.Fori(1, steps // UNROLL - 1) as r:
        for s in range(UNROLL):
            body(eng.snap(r * UNROLL + s), s)
    for s in range(UNROLL):
        body(steps - UNROLL + s, s)


def wait_past(eng, sem, value):
    if not isinstance(value, int) or value > 0:
        eng.wait_ge(sem, value)


def in_slot(q, slot, slots, per):
    return (q - slot) * (per // slots) + (slot // slots + 1) * per


def build_gnn(nc, x, src_col, dst_col, dst_row, edge_t, w0_t, b0, w1ab, w1c, b1, w2, b2, w3, b3, out):
    N, F = out.shape
    NB = x.shape[0] // P
    NP = NB * P
    NPP = NP + P
    TP = src_col.shape[1]
    NG = TP // GROUP
    W = GROUP * P
    WH = W // 2
    EF = edge_t.shape[0]
    H = w2.shape[0]
    CB = divisor(NB, 7)
    NK = NB // CB
    HC = divisor(TP, 16)
    CHUNKS = TP // HC
    GP = divisor(NG, P)
    GK = NG // GP
    assert NG % UNROLL == 0 and NG >= 3 * UNROLL and H == P

    def dram(name, shape, dt):
        return nc.dram_tensor(name, shape, dt).ap()

    sum_tab = [dram(f"sum_tab{j}", [NPP, F], F32) for j in range(TABLES)]
    g_tab = dram("g_tab", [NPP, PLANES * F], BF16)
    p_tab = dram("p_tab", [NPP, PLANES * H], BF16)
    q_tab = dram("q_tab", [NPP, PLANES * H], BF16)
    ext_tab = dram("ext_tab", [2, NG], F32)
    cnt_tab = dram("cnt_tab", [1, NPP], F32)

    def node_view(table):
        return table[0:NP, :].rearrange("(b p) f -> p b f", p=P)

    with ExitStack() as whole:
        def sb(name, shape, dt, ctx=whole):
            return ctx.enter_context(nc.sbuf_tensor(name, shape, dt))

        def ps(name, shape, dt, ctx):
            return ctx.enter_context(nc.psum_tensor(name, shape, dt))

        def sem(name, ctx=whole):
            return ctx.enter_context(nc.semaphore(name))

        src_f = sb("src_f", [P, TP], F32)
        dst_f = sb("dst_f", [P, TP], F32)
        lo_b = sb("lo_b", [P, TP], BF16)
        hi_b = sb("hi_b", [P, TP], BF16)
        x1 = sb("x1", [P, NB, F], F32)
        act_in = sb("act_in", [P, NB, F], F32)
        base_col = sb("base_col", [P, NG], F32)
        sched = sb("sched", [1, 3, NG], I32)
        block_base = sb("block_base", [P, NB + 1], F32)
        iota_row = sb("iota_row", [P, P], F32)
        iota_b = sb("iota_b", [P, P], BF16)
        ident_f = sb("ident_f", [P, P], F32)
        ident_b = sb("ident_b", [P, P], BF16)
        ident_hi = sb("ident_hi", [P, P], BF16)
        ones_b = sb("ones_b", [P, 1], BF16)
        zero_b = sb("zero_b", [P, PLANES * H], BF16)
        below = sb("below", [P, P], F32)
        trash = sb("trash", [P, 1], F32)
        deg_is = sb("deg_is", [P, NB], F32)
        dst_cnt = sb("dst_cnt", [P, NB], F32)
        half = sb("half", [P, NB], F32)
        stat = sb("stat", [P, NB], F32)

        def linker(eng, chain):
            count = [0]

            def link(ins):
                count[0] += 1
                ins.then_inc(chain, 1)
                eng.wait_ge(chain, count[0])
            return link

        def layer_norm(dve, link, pool_pow, a, scratch):
            link(dve.tensor_reduce(stat[:, :], a, AX.X, ALU.add))
            link(dve.tensor_scalar(stat[:, :], stat[:, :], 1.0 / F, None, ALU.mult))
            link(dve.tensor_tensor(act_in[:, :, :], a, stat[:, :].unsqueeze(2).to_broadcast([P, NB, F]), ALU.subtract))
            link(dve.tensor_tensor(scratch, act_in[:, :, :], act_in[:, :, :], ALU.mult))
            link(dve.tensor_reduce(stat[:, :], scratch, AX.X, ALU.add))
            link(dve.tensor_scalar(stat[:, :], stat[:, :], 1.0 / F, EPS, ALU.mult, ALU.add))
            pool_pow()
            link(dve.tensor_tensor(act_in[:, :, :], act_in[:, :, :],
                                   stat[:, :].unsqueeze(2).to_broadcast([P, NB, F]), ALU.mult))
            link(dve.tensor_scalar(act_in[:, :, :], act_in[:, :, :], 0.0, None, ALU.max))

        def load_base(eng, q):
            return eng.value_load(sched[0:1, 0, bass.ds(q, 1)], min_val=0, max_val=NP - P)

        def each_extra(eng, q, body):
            extra = eng.value_load(sched[0:1, 1, bass.ds(q, 1)], min_val=0, max_val=NB)
            with eng.If(extra > 0):
                before = eng.value_load(sched[0:1, 2, bass.ds(q, 1)], min_val=0, max_val=NB * NG)
                base = load_base(eng, q)
                with eng.Fori(0, extra) as x:
                    first = eng.snap(nc.s_assert_within(base + (x + 1) * P, 0, NP))
                    body(eng.snap(before + x), first, x)

        def one_hots(dve, hot, q, dst=None):
            iota = iota_b if hot.dtype == BF16 else iota_row
            for j in range(GROUP):
                at = dst_f[:, bass.ds(q * GROUP + j, 1)] if dst is None else dst[:, j:j + 1]
                last = dve.tensor_scalar(hot[:, j, :], iota[:, :], base_col[:, bass.ds(q, 1)], at,
                                         ALU.add, ALU.is_equal)
            return last

        with ExitStack() as ctx:
            src_i = sb("src_i", [P, TP], I32, ctx)
            dst_i = sb("dst_i", [P, TP], I32, ctx)
            hot_lo = [sb(f"hot_lo{k}", [P, HC, P], BF16, ctx) for k in range(2)]
            hot_hi = [sb(f"hot_hi{k}", [P, HC, NB], BF16, ctx) for k in range(2)]
            scratch = sb("scratch", [P, NB, F], F32, ctx)
            late = sb("late", [P, max(NB * PLANES * F, 2 * GK * W)], BF16, ctx)
            g_planes = late[:, 0:NB * PLANES * F].rearrange("p (b f) -> p b f", b=NB)
            row_view = late[0:GP, 0:2 * GK * W].bitcast(I32).rearrange("p (k e) -> p k e", k=GK)
            hi_f = src_i[:, :].bitcast(F32)
            lo_f = dst_i[:, :].bitcast(F32)
            ext = sb("ext", [GP, 2, GK], F32, ctx)
            ext_bc = sb("ext_bc", [P, 2, NG], F32, ctx)
            scan = [sb(f"scan{k}", [1, NG], F32, ctx) for k in range(2)]
            extra_i = sb("extra_i", [1, NG], I32, ctx)
            extra_f = sb("extra_f", [1, NG], F32, ctx)
            hist = ps("hist", [P, NB], F32, ctx)

            loaded = sem("loaded", ctx)
            x_loaded = sem("x_loaded", ctx)
            row_loaded = sem("row_loaded", ctx)
            const_ready = sem("const_ready", ctx)
            hot_ready = sem("hot_ready", ctx)
            hot_used = sem("hot_used", ctx)
            ext_ready = sem("ext_ready", ctx)
            ext_saved = sem("ext_saved", ctx)
            ext_loaded = sem("ext_loaded", ctx)
            zero_ready = sem("zero_ready", ctx)
            zeroed = sem("zeroed", ctx)
            g_ready = sem("g_ready", ctx)
            g_saved = sem("g_saved", ctx)
            pow_ask = sem("pow_ask", ctx)
            pow_done = sem("pow_done", ctx)
            chain = sem("chain", ctx)
            pool_chain = sem("pool_chain", ctx)
            block = ctx.enter_context(nc.Block())

            @block.sync
            def _(sp):
                sp.dma_start(src_i[:, :], src_col).then_inc(loaded, 16)
                sp.dma_start(dst_i[:, :], dst_col).then_inc(loaded, 16)
                sp.dma_start(row_view, dst_row.rearrange("(p k) e -> p k e", k=GK)).then_inc(row_loaded, 16)
                sp.dma_start(x1[:, :, :], x.rearrange("(b p) f -> p b f", p=P)).then_inc(x_loaded, 16)
                sp.wait_ge(ext_ready, 1)
                for k in range(2):
                    sp.dma_start(ext_tab[k:k + 1, :].rearrange("o (p k) -> p (o k)", k=GK),
                                 ext[:, k, :]).then_inc(ext_saved, 16)
                sp.wait_ge(ext_saved, 32)
                sp.dma_start(ext_bc[:, :, :], ext_tab.unsqueeze(0).to_broadcast([P, 2, NG])).then_inc(ext_loaded, 16)
                sp.wait_ge(const_ready, 1)
                sp.dma_start(g_tab[NP:NPP, :], zero_b[:, 0:PLANES * F]).then_inc(g_saved, 16)
                sp.dma_start(q_tab[NP:NPP, :], zero_b[:, :]).then_inc(g_saved, 16)
                sp.dma_start(p_tab[NP:NPP, :], zero_b[:, :]).then_inc(g_saved, 16)
                sp.wait_ge(g_ready, 1)
                sp.dma_start(node_view(g_tab), g_planes).then_inc(g_saved, 16)
                sp.wait_ge(g_saved, 64)

            @block.scalar
            def _(act):
                act.wait_ge(zero_ready, 1)
                for j in range(TABLES):
                    act.dma_start(node_view(sum_tab[j]), scratch[:, :, :]).then_inc(zeroed, 16)
                    act.dma_start(sum_tab[j][NP:NPP, :], scratch[:, 0, :]).then_inc(zeroed, 16)
                act.wait_ge(zeroed, 32 * TABLES)

            @block.gpsimd
            def _(pool):
                link = linker(pool, pool_chain)
                pool.memset(scratch[:, :, :], 0.0).then_inc(zero_ready, 1)

                def iota(dst, steps, base, by_partition):
                    return pool.iota(dst, steps, base=base, channel_multiplier=by_partition,
                                     allow_small_or_imprecise_dtypes=True)

                iota(iota_row[:, :], [[1, P]], 0, 0)
                iota(iota_b[:, :], [[1, P]], 0, 0)
                iota(block_base[:, :], [[P, NB + 1]], 0, 0)
                iota(trash[:, :], [[0, 1]], NP, 1)
                pool.memset(half[:, :], -0.5)
                pool.memset(ones_b[:, :], 1.0)
                pool.memset(zero_b[:, :], 0.0)
                for m in (ident_f, below):
                    link(pool.memset(m[:, :], 0.0))
                link(pool.affine_select(ident_f[:, :], ident_f[:, :], [[-1, P]], ALU.not_equal, 1.0,
                                        base=0, channel_multiplier=1))
                link(pool.affine_select(below[:, :], below[:, :], [[1, P]], ALU.is_ge, 1.0,
                                        base=0, channel_multiplier=-1))
                link(pool.tensor_copy(ident_b[:, :], ident_f[:, :]))
                pool.tensor_scalar(ident_hi[:, :], ident_f[:, :], float(P), None, ALU.mult).then_inc(const_ready, 1)
                for step in range(2):
                    a = (stat, deg_is)[step]
                    pool.wait_ge(pow_ask, step + 1)
                    pool.tensor_tensor(a[:, :], a[:, :], half[:, :], ALU.pow).then_inc(pow_done, 1)

            @block.tensor
            def _(pe):
                def count_chunk(n, k):
                    pe.wait_ge(hot_ready, n + 1)
                    for c in range(HC):
                        last = pe.matmul(hist[:, :], hot_lo[k][:, c, :], hot_hi[k][:, c, :],
                                         start=False, stop=False, skip_group_check=True)
                    last.then_inc(hot_used, 1)

                pe.wait_ge(const_ready, 1)
                pe.matmul(hist[:, :], zero_b[:, 0:P], zero_b[:, 0:NB], start=True, stop=False, skip_group_check=True)
                pe.sem_inc(hot_used, 2)
                with pe.Fori(0, CHUNKS // 2) as r:
                    count_chunk(r * 2, 0)
                    count_chunk(r * 2 + 1, 1)
                if CHUNKS % 2:
                    count_chunk(CHUNKS - 1, 0)

            @block.vector
            def _(dve):
                link = linker(dve, chain)
                dve.wait_ge(loaded, 32)
                link(dve.tensor_copy(src_f[:, :], src_i[:, :]))
                link(dve.tensor_copy(dst_f[:, :], dst_i[:, :]))
                link(dve.tensor_scalar(dst_i[:, :], src_i[:, :], P - 1, None, ALU.bitwise_and))
                link(dve.tensor_scalar(src_i[:, :], src_i[:, :], P.bit_length() - 1, None, ALU.logical_shift_right))
                link(dve.tensor_copy(lo_f, dst_i[:, :]))
                link(dve.tensor_copy(hi_f, src_i[:, :]))
                link(dve.tensor_copy(lo_b[:, :], lo_f))
                link(dve.tensor_copy(hi_b[:, :], hi_f))

                dve.wait_ge(row_loaded, 16)
                dve.tensor_reduce(ext[:, 0, :], row_view, AX.X, ALU.min)
                dve.tensor_reduce(ext[:, 1, :], row_view, AX.X, ALU.max).then_inc(ext_ready, 1)

                def hot_chunk(n, k):
                    dve.wait_ge(hot_used, n + 1)
                    for c in range(HC):
                        t = bass.ds(n * HC + c, 1)
                        dve.tensor_scalar(hot_lo[k][:, c, :], iota_b[:, :], lo_f[:, t], None, ALU.is_equal)
                        last = dve.tensor_scalar(hot_hi[k][:, c, :], iota_b[:, 0:NB], hi_f[:, t], None, ALU.is_equal)
                    last.then_inc(hot_ready, 1)

                dve.wait_ge(const_ready, 1)
                with dve.Fori(0, CHUNKS // 2) as r:
                    hot_chunk(r * 2, 0)
                    hot_chunk(r * 2 + 1, 1)
                if CHUNKS % 2:
                    hot_chunk(CHUNKS - 1, 0)

                dve.wait_ge(ext_loaded, 16)
                link(dve.tensor_scalar(base_col[:, :], ext_bc[:, 0, :], float(NP - P), None, ALU.min))
                link(dve.tensor_copy(sched[:, 0, :], base_col[0:1, :]))
                link(dve.scalar_tensor_tensor(extra_i[:, :], ext_bc[0:1, 1, :], float(N - 1), base_col[0:1, :],
                                              ALU.min, ALU.subtract))
                link(dve.tensor_scalar(sched[:, 1, :], extra_i[:, :], P.bit_length() - 1, None,
                                       ALU.logical_shift_right))
                link(dve.tensor_copy(extra_f[:, :], sched[:, 1, :]))
                link(dve.tensor_copy(scan[0][:, :], sched[:, 1, :]))
                d, k = 1, 0
                while d < NG:
                    link(dve.tensor_tensor(scan[1 - k][:, d:], scan[k][:, d:], scan[k][:, 0:NG - d], ALU.add))
                    link(dve.tensor_copy(scan[1 - k][:, 0:d], scan[k][:, 0:d]))
                    d, k = 2 * d, 1 - k
                link(dve.tensor_tensor(sched[:, 2, :], scan[k][:, :], extra_f[:, :], ALU.subtract))

                dve.wait_ge(x_loaded, 16)
                dve.wait_ge(zeroed, 32 * TABLES)

                def power(step):
                    def go():
                        dve.sem_inc(pow_ask, 1)
                        dve.wait_ge(pow_done, step)
                    return go

                layer_norm(dve, link, power(1), x1[:, :, :], scratch[:, :, :])
                dve.wait_ge(hot_used, CHUNKS + 2)
                link(dve.tensor_scalar(deg_is[:, :], hist[:, :], 1.0, None, ALU.max))
                power(2)()
                link(dve.scalar_tensor_tensor(deg_is[:, :], hist[:, :], 0.0, deg_is[:, :], ALU.is_gt, ALU.mult))
                link(dve.tensor_tensor(scratch[:, :, :], act_in[:, :, :],
                                       deg_is[:, :].unsqueeze(2).to_broadcast([P, NB, F]), ALU.mult))
                for m in range(PLANES):
                    plane = g_planes[:, :, m * F:(m + 1) * F]
                    link(dve.tensor_copy(plane, scratch[:, :, :]))
                    if m < PLANES - 1:
                        link(dve.tensor_tensor(scratch[:, :, :], scratch[:, :, :], plane, ALU.subtract))
                dve.sem_inc(g_ready, 1)

        with ExitStack() as ctx:
            hot = [sb(f"hot{k}", [P, GROUP, P], BF16, ctx) for k in range(2)]
            hot_t = sb("hot_t", [P, W], BF16, ctx)
            g_win = [sb(f"g_win{k}", [P, PLANES * F], BF16, ctx) for k in range(2)]
            same = [sb(f"same{k}", [P, GROUP, P], F32, ctx) for k in range(2)]
            junk = sb("junk", [P, GROUP, P], F32, ctx)
            dup = sb("dup", [P, GROUP], F32, ctx)
            moved = sb("moved", [P, GROUP], F32, ctx)
            rows = sb("rows", [P, GROUP, F], F32, ctx)
            vals = [sb(f"vals{k}", [P, GROUP, F], F32, ctx) for k in range(2)]
            idx = [sb(f"idx{k}", [P, GROUP], I32, ctx) for k in range(2)]
            cnt_acc = sb("cnt_acc", [1, NPP], F32, ctx)
            x_dst = sb("x_dst", [P, GROUP], F32, ctx)
            x_hot = sb("x_hot", [P, GROUP, P], BF16, ctx)
            x_hot_t = sb("x_hot_t", [P, W], BF16, ctx)
            x_g = sb("x_g", [P, PLANES * F], BF16, ctx)
            t_ps = ps("t_ps", [P, W], BF16, ctx)
            cnt_ps = ps("cnt_ps", [1, P], F32, ctx)
            src_ps = ps("src_ps", [P, W], F32, ctx)
            rows_ps = ps("rows_ps", [P, GROUP * F], F32, ctx)
            comb_ps = ps("comb_ps", [P, GROUP, F], F32, ctx)
            x_t_ps = ps("x_t_ps", [P, W], BF16, ctx)
            x_cnt_ps = ps("x_cnt_ps", [1, P], F32, ctx)

            hot_ready = sem("hot_ready_b", ctx)
            t_made = sem("t_made_b", ctx)
            hot_t_ready = sem("hot_t_ready", ctx)
            g_loaded = [sem(f"g_loaded{k}", ctx) for k in range(2)]
            rows_made = sem("rows_made", ctx)
            rows_kept = sem("rows_kept", ctx)
            same_ready = sem("same_ready", ctx)
            comb_made = sem("comb_made", ctx)
            vals_ready = sem("vals_ready", ctx)
            idx_ready = sem("idx_ready", ctx)
            cnt_added = sem("cnt_added", ctx)
            dup_steps = sem("dup_steps", ctx)
            cnt_zero = sem("cnt_zero", ctx)
            cnt_done = sem("cnt_done", ctx)
            cnt_saved = sem("cnt_saved", ctx)
            scattered = [sem(f"scattered{j}", ctx) for j in range(TABLES)]
            sp_turns = sem("sp_turns", ctx)
            pool_turns = sem("pool_turns", ctx)
            pe_turns = sem("pe_turns", ctx)
            dve_turns = sem("dve_turns", ctx)
            x_dst_ready = sem("x_dst_ready", ctx)
            x_hot_ready = sem("x_hot_ready", ctx)
            x_t_made = sem("x_t_made", ctx)
            x_hot_t_ready = sem("x_hot_t_ready", ctx)
            x_loaded = sem("x_loaded_b", ctx)
            x_used = sem("x_used", ctx)
            x_added = sem("x_added", ctx)
            block = ctx.enter_context(nc.Block())
            STEPS = 2

            @block.sync
            def _(sp):
                def step(q, s):
                    wait_past(sp, rows_made, q - 1)
                    sp.sem_inc(sp_turns, 1)
                    base = load_base(sp, q)
                    sp.dma_start(g_win[s % 2][:, :], g_tab[bass.ds(base, P), :]).then_inc(g_loaded[s % 2], 16)

                    def more(e, first, x):
                        sp.wait_ge(x_used, e + 1)
                        sp.sem_inc(sp_turns, 1)
                        sp.dma_start(x_g[:, :], g_tab[bass.ds(first, P), :]).then_inc(x_loaded, 16)
                    each_extra(sp, q, more)

                paced(sp, NG, step)
                sp.wait_ge(cnt_done, 1)
                sp.dma_start(cnt_tab, cnt_acc[:, :]).then_inc(cnt_saved, 16)
                sp.wait_ge(cnt_saved, 16)

            @block.scalar
            def _(act):
                def keep_hot_t(q):
                    act.wait_ge(t_made, q + 1)
                    wait_past(act, rows_made, q)
                    act.copy(hot_t[:, :], t_ps[:, :]).then_inc(hot_t_ready, 1)

                keep_hot_t(0)

                def step(q, s):
                    def more(e, first, x):
                        act.wait_ge(x_t_made, e + 1)
                        act.copy(x_hot_t[:, :], x_t_ps[:, :]).then_inc(x_hot_t_ready, 1)
                    each_extra(act, q, more)
                    act.wait_ge(rows_made, q + 1)
                    wait_past(act, comb_made, q)
                    act.copy(rows[:, :, :].rearrange("p g f -> p (g f)"), rows_ps[:, :]).then_inc(rows_kept, 1)
                    if not isinstance(q, int) or q + 1 < NG:
                        keep_hot_t(q + 1)
                    act.wait_ge(comb_made, q + 1)
                    for j in range(TABLES):
                        wait_past(act, scattered[j], (q - 1) * 16)
                    act.copy(vals[s % 2][:, :, :], comb_ps[:, :, :]).then_inc(vals_ready, 1)

                paced(act, NG, step)

            @block.tensor
            def _(pe):
                def front(q, k):
                    pe.wait_ge(hot_ready, q + 1)
                    wait_past(pe, hot_t_ready, q)
                    pe.sem_inc(pe_turns, 1)
                    for j in range(GROUP):
                        pe.transpose(t_ps[:, j * P:(j + 1) * P], hot[k][:, j, :], ident_b[:, :])
                    wait_past(pe, cnt_added, q)
                    for j in range(GROUP):
                        pe.matmul(cnt_ps[:, :], ones_b[:, :], hot[k][:, j, :], start=(j == 0), stop=(j == GROUP - 1))
                    wait_past(pe, same_ready, q)
                    for j in range(GROUP):
                        t = bass.ds(q * GROUP + j, 1)
                        pe.matmul(src_ps[:, j * P:(j + 1) * P], hi_b[:, t].to_broadcast([P, P]), ident_hi[:, :],
                                  start=True, stop=False)
                        last = pe.matmul(src_ps[:, j * P:(j + 1) * P], lo_b[:, t].to_broadcast([P, P]), ident_b[:, :],
                                         start=False, stop=True)
                    last.then_inc(t_made, 1)

                def gather(hots, g):
                    for j in range(GROUP):
                        for m in range(PLANES):
                            last = pe.matmul(rows_ps[:, j * F:(j + 1) * F], hots[:, j * P:(j + 1) * P],
                                             g[:, m * F:(m + 1) * F], start=False, stop=False, skip_group_check=True)
                    return last

                pe.sem_inc(x_used, 1)
                front(0, 0)

                def step(q, s):
                    k = s % 2
                    wait_past(pe, rows_kept, q)
                    pe.matmul(rows_ps[:, :], zero_b[:, 0:P], zero_b[:, 0:GROUP * F], start=True, stop=False,
                              skip_group_check=True)

                    def more(e, first, x):
                        pe.wait_ge(x_hot_ready, e + 1)
                        pe.sem_inc(pe_turns, 1)
                        for j in range(GROUP):
                            pe.transpose(x_t_ps[:, j * P:(j + 1) * P], x_hot[:, j, :], ident_b[:, :])
                        for j in range(GROUP):
                            last = pe.matmul(x_cnt_ps[:, :], ones_b[:, :], x_hot[:, j, :], start=(j == 0),
                                             stop=(j == GROUP - 1))
                        last.then_inc(x_t_made, 1)
                        pe.wait_ge(x_hot_t_ready, e + 1)
                        pe.wait_ge(x_loaded, e * 16 + 16)
                        gather(x_hot_t, x_g).then_inc(x_used, 1)
                    each_extra(pe, q, more)
                    pe.wait_ge(hot_t_ready, q + 1)
                    pe.wait_ge(g_loaded[k], in_slot(q, s, 2, 16))
                    gather(hot_t, g_win[k]).then_inc(rows_made, 1)
                    if not isinstance(q, int) or q + 1 < NG:
                        front(q + 1, 1 - k)
                    pe.wait_ge(same_ready, q + 1)
                    pe.wait_ge(rows_kept, q + 1)
                    wait_past(pe, vals_ready, q)
                    for j in range(GROUP):
                        last = pe.matmul(comb_ps[:, j, :], same[k][:, j, :], rows[:, j, :], start=True, stop=True)
                    last.then_inc(comb_made, 1)

                paced(pe, NG, step)

            @block.vector
            def _(dve):
                dve.memset(cnt_acc[:, :], 0.0).then_inc(cnt_zero, 1)
                dve.memset(junk[:, :, :], 0.0)
                dve.wait_ge(cnt_zero, 1)
                one_hots(dve, hot[0], 0).then_inc(hot_ready, 1)

                def add_count(first, counts):
                    at = cnt_acc[0:1, bass.ds(first, P)]
                    return dve.tensor_tensor(at, at, counts[:, :], ALU.add)

                def step(q, s):
                    k = s % 2
                    if not isinstance(q, int) or q + 1 < NG:
                        wait_past(dve, t_made, q)
                        one_hots(dve, hot[1 - k], q + 1).then_inc(hot_ready, 1)
                    wait_past(dve, comb_made, q - 1)
                    dve.wait_ge(t_made, q + 1)
                    for j in range(GROUP):
                        last = dve.tensor_scalar(same[k][:, j, :], src_ps[:, j * P:(j + 1) * P],
                                                 src_f[:, bass.ds(q * GROUP + j, 1)], None, ALU.is_equal)
                    last.then_inc(same_ready, 1)
                    wait_past(dve, cnt_added, q)
                    add_count(load_base(dve, q), cnt_ps).then_inc(cnt_added, 1)

                    def more(e, first, x):
                        dve.tensor_scalar(x_dst[:, :], dst_f[:, bass.ds(q * GROUP, GROUP)],
                                          block_base[:, bass.ds(x + 1, 1)], None, ALU.subtract
                                          ).then_inc(x_dst_ready, 1)
                        dve.wait_ge(x_dst_ready, e + 1)
                        one_hots(dve, x_hot, q, x_dst).then_inc(x_hot_ready, 1)
                        dve.wait_ge(cnt_added, q + 1)
                        dve.wait_ge(x_t_made, e + 1)
                        add_count(first, x_cnt_ps).then_inc(x_added, 1)
                        dve.wait_ge(x_added, e + 1)
                    each_extra(dve, q, more)
                    dve.wait_ge(same_ready, q + 1)
                    dve.sem_inc(dve_turns, 1)
                    for j in range(GROUP):
                        last = dve.tensor_tensor_reduce(junk[:, j, :], same[k][:, j, :], below[:, :], 1.0, 0.0,
                                                        ALU.mult, ALU.max, dup[:, j:j + 1])
                    last.then_inc(dup_steps, 1)
                    dve.wait_ge(dup_steps, q * STEPS + 1)
                    dve.scalar_tensor_tensor(moved[:, :], src_f[:, bass.ds(q * GROUP, GROUP)], trash[:, 0:1],
                                             dup[:, :], ALU.subtract, ALU.mult).then_inc(dup_steps, 1)
                    for j in range(TABLES):
                        wait_past(dve, scattered[j], (q - 1) * 16)
                    dve.wait_ge(dup_steps, q * STEPS + 2)
                    dve.tensor_tensor(idx[k][:, :], src_f[:, bass.ds(q * GROUP, GROUP)], moved[:, :],
                                      ALU.subtract).then_inc(idx_ready, 1)

                paced(dve, NG, step)
                dve.wait_ge(cnt_added, NG)
                dve.sem_inc(cnt_done, 1)

            @block.gpsimd
            def _(pool):
                def step(q, s):
                    pool.wait_ge(vals_ready, q + 1)
                    pool.wait_ge(idx_ready, q + 1)
                    for j in range(TABLES):
                        wait_past(pool, scattered[j], q * 16)
                        pool.sem_inc(pool_turns, 1)
                        pool.indirect_dma_start(sum_tab[j], bass.IndirectOffsetOnAxis(idx[s % 2][:, j:j + 1], 0),
                                                vals[s % 2][:, j, :], None, compute_op=ALU.add
                                                ).then_inc(scattered[j], 16)

                paced(pool, NG, step)
                for j in range(TABLES):
                    pool.wait_ge(scattered[j], NG * 16)

        nb2 = sb("nb2", [P, H], F32)
        b1_col = sb("b1_col", [H, 1], F32)
        w1c_sb = sb("w1c_sb", [P, H], F32)
        w2_sb = sb("w2_sb", [H, H], F32)
        w3_sb = sb("w3_sb", [H, F], F32)
        c_bc = sb("c_bc", [P, F], F32)
        with ExitStack() as ctx:
            sums = [sb(f"sums{j}", [P, NB, F], F32, ctx) for j in range(TABLES)]
            w0_sb = sb("w0_sb", [F, F], F32, ctx)
            w1_sb = sb("w1_sb", [F, 2 * H], F32, ctx)
            b0_bc = sb("b0_bc", [P, F], F32, ctx)
            b3_bc = sb("b3_bc", [P, F], F32, ctx)
            cnt_rows = sb("cnt_rows", [NB, P], F32, ctx)
            b2_col = sb("b2_col", [H, 1], F32, ctx)
            blk = sb("blk", [P, CB, F], F32, ctx)
            blk_t = sb("blk_t", [F, CB, P], F32, ctx)
            y = sb("y", [P, CB, F], F32, ctx)
            rest = sb("rest", [P, CB, 2 * H], F32, ctx)
            p_out = sb("p_out", [P, CB, PLANES, H], BF16, ctx)
            q_out = sb("q_out", [P, CB, PLANES, H], BF16, ctx)
            t_ps = ps("t_ps_c", [F, 8, P], F32, ctx)
            y_ps = ps("y_ps", [P, CB, F], F32, ctx)
            pq_ps = ps("pq_ps", [P, 8, 2 * H], F32, ctx)
            c_ps = ps("c_ps", [P, F + NB], F32, ctx)

            sum_loaded = [sem(f"sum_loaded{j}", ctx) for j in range(TABLES)]
            cnt_loaded = sem("cnt_loaded", ctx)
            summed = sem("summed", ctx)
            w_loaded = sem("w_loaded", ctx)
            chain = sem("chain_c", ctx)
            blk_ready = sem("blk_ready", ctx)
            t_made = sem("t_made", ctx)
            t_ready = sem("t_ready", ctx)
            y_made = sem("y_made", ctx)
            c_made = sem("c_made", ctx)
            plane_ready = sem("plane_ready", ctx)
            planes_free = sem("planes_free", ctx)
            planes_stored = sem("planes_stored", ctx)
            pow_ask = sem("pow_ask_c", ctx)
            pow_done = sem("pow_done_c", ctx)
            rest_ready = sem("rest_ready", ctx)
            w1c_zero = sem("w1c_zero", ctx)
            y_ready = sem("y_ready", ctx)
            turns = sem("turns_c", ctx)
            x1_ready = sem("x1_ready", ctx)
            block = ctx.enter_context(nc.Block())

            @block.sync
            def _(sp):
                for j in range(TABLES):
                    sp.dma_start(sums[j][:, :, :], node_view(sum_tab[j])).then_inc(sum_loaded[j], 16)
                sp.dma_start(w0_sb[:, :], w0_t).then_inc(w_loaded, 16)
                sp.dma_start(w1_sb[:, :], w1ab).then_inc(w_loaded, 16)
                sp.dma_start(w2_sb[:, :], w2).then_inc(w_loaded, 16)
                sp.dma_start(w3_sb[:, :], w3).then_inc(w_loaded, 16)
                sp.dma_start(b0_bc[:, :], b0.to_broadcast([P, F])).then_inc(w_loaded, 16)
                sp.dma_start(b3_bc[:, :], b3.to_broadcast([P, F])).then_inc(w_loaded, 16)
                sp.dma_start(nb2[:, :], b2.to_broadcast([P, H])).then_inc(w_loaded, 16)
                sp.dma_start(b1_col[:, :], b1).then_inc(w_loaded, 16)
                sp.dma_start(b2_col[:, :], b2.rearrange("o h -> h o")).then_inc(w_loaded, 16)
                sp.wait_ge(w1c_zero, 1)
                sp.dma_start(w1c_sb[0:EF, :], w1c).then_inc(w_loaded, 16)
                sp.dma_start(cnt_rows[:, :], cnt_tab[0:1, 0:NP].rearrange("o (b p) -> (o b) p", p=P)
                             ).then_inc(cnt_loaded, 16)
                sp.sem_inc(planes_free, 1)
                with sp.Fori(0, NK) as k:
                    blocks = bass.ds(k * CB, CB)
                    sp.wait_ge(plane_ready, (k + 1) * 2 * PLANES)
                    for table, out_planes in ((p_tab, p_out), (q_tab, q_out)):
                        sp.dma_start(node_view(table)[:, blocks, :],
                                     out_planes[:, :, :, :].rearrange("p b k h -> p b (k h)")
                                     ).then_inc(planes_stored, 16)
                    sp.wait_ge(planes_stored, k * 32 + 32)
                    sp.sem_inc(planes_free, 1)

            W_LOADS = 10

            @block.gpsimd
            def _(pool):
                pool.memset(w1c_sb[:, :], 0.0).then_inc(w1c_zero, 1)
                pool.wait_ge(pow_ask, 1)
                pool.tensor_tensor(stat[:, :], stat[:, :], half[:, :], ALU.pow).then_inc(pow_done, 1)

            @block.tensor
            def _(pe):
                pe.wait_ge(w_loaded, 16 * W_LOADS)
                pe.matmul(c_ps[:, 0:F], b2_col[:, 0:1].to_broadcast([H, P]), w3_sb[:, :], start=True,
                          stop=True)
                pe.wait_ge(cnt_loaded, 16)
                pe.transpose(c_ps[:, F:F + NB], cnt_rows[:, :], ident_f[0:NB, 0:NB]).then_inc(c_made, 1)

                def turn(n):
                    pe.wait_ge(blk_ready, n + 1)
                    pe.sem_inc(turns, 1)
                    for c in range(CB):
                        last = pe.transpose(t_ps[:, c, :], blk[:, c, :], ident_f[:, :])
                    last.then_inc(t_made, 1)
                    pe.wait_ge(t_ready, n + 1)

                with pe.Fori(0, NK) as k:
                    turn(k)
                    for c in range(CB):
                        last = pe.matmul(y_ps[:, c, :], blk_t[:, c, :], w0_sb[:, :], start=True, stop=True)
                    last.then_inc(y_made, 1)
                with pe.Fori(0, NK) as k:
                    turn(k + NK)
                    for c in range(CB):
                        last = pe.matmul(pq_ps[:, c, :], blk_t[:, c, :], w1_sb[:, :], start=True, stop=True)
                    last.then_inc(y_made, 1)

            @block.scalar
            def _(act):
                with act.Fori(0, NK) as k:
                    act.wait_ge(t_made, k + 1)
                    act.copy(blk_t[:, :, :], t_ps[:, 0:CB, :]).then_inc(t_ready, 1)
                with act.Fori(0, NK) as k:
                    act.wait_ge(t_made, k + (NK + 1))
                    act.copy(blk_t[:, :, :], t_ps[:, 0:CB, :]).then_inc(t_ready, 1)
                    act.wait_ge(y_made, k + (NK + 1))
                    act.wait_ge(planes_free, k + 1)
                    for m in range(PLANES):
                        if m:
                            act.wait_ge(rest_ready, k * (PLANES - 1) + m)
                        v = pq_ps[:, 0:CB, :] if m == 0 else rest[:, :, :]
                        act.copy(p_out[:, :, m, :], v[:, :, 0:H]).then_inc(plane_ready, 1)
                        act.copy(q_out[:, :, m, :], v[:, :, H:2 * H]).then_inc(plane_ready, 1)

            @block.vector
            def _(dve):
                link = linker(dve, chain)
                dve.wait_ge(sum_loaded[0], 16)
                for j in range(1, TABLES):
                    dve.wait_ge(sum_loaded[j], 16)
                    dve.tensor_tensor(sums[0][:, :, :], sums[0][:, :, :], sums[j][:, :, :], ALU.add).then_inc(summed, 1)
                    dve.wait_ge(summed, j)
                dve.wait_ge(w_loaded, 16 * W_LOADS)
                link(dve.tensor_scalar(nb2[:, :], nb2[:, :], -1.0, None, ALU.mult))
                dve.wait_ge(c_made, 1)
                dve.tensor_copy(dst_cnt[:, :], c_ps[:, F:F + NB])
                link(dve.tensor_tensor(c_bc[:, :], c_ps[:, 0:F], b3_bc[:, :], ALU.add))
                with dve.Fori(0, NK) as k:
                    blocks = bass.ds(k * CB, CB)
                    dve.tensor_tensor(blk[:, :, :], sums[0][:, blocks, :],
                                      deg_is[:, blocks].unsqueeze(2).to_broadcast([P, CB, F]),
                                      ALU.mult).then_inc(blk_ready, 1)
                    dve.wait_ge(y_made, k + 1)
                    dve.tensor_tensor(y[:, :, :], y_ps[:, :, :], b0_bc[:, :].unsqueeze(1).to_broadcast([P, CB, F]),
                                      ALU.add).then_inc(y_ready, 1)
                    dve.wait_ge(y_ready, k + 1)
                    dve.scalar_tensor_tensor(x1[:, blocks, :], y[:, :, :], 0.0, x1[:, blocks, :], ALU.max,
                                             ALU.add).then_inc(x1_ready, 1)
                dve.wait_ge(x1_ready, NK)

                def power():
                    dve.sem_inc(pow_ask, 1)
                    dve.wait_ge(pow_done, 1)

                layer_norm(dve, link, power, x1[:, :, :], sums[0][:, :, :])
                with dve.Fori(0, NK) as k:
                    blocks = bass.ds(k * CB, CB)
                    dve.tensor_copy(blk[:, :, :], act_in[:, blocks, :]).then_inc(blk_ready, 1)
                    for m in range(PLANES - 1):
                        dve.wait_ge(plane_ready, k * 2 * PLANES + 2 * m + 2)
                        v = pq_ps[:, 0:CB, :] if m == 0 else rest[:, :, :]
                        for w, pl in ((0, p_out[:, :, m, :]), (1, q_out[:, :, m, :])):
                            last = dve.tensor_tensor(rest[:, :, w * H:(w + 1) * H], v[:, :, w * H:(w + 1) * H], pl,
                                                     ALU.subtract)
                        last.then_inc(rest_ready, 1)

        seg_acc = sb("seg_acc", [H, NPP], F32)
        with ExitStack() as ctx:
            idx = [sb(f"idx_d{s}", [P, GROUP], I32, ctx) for s in range(UNROLL)]
            p_got = [sb(f"p_got{s}", [P, GROUP, PLANES * H], BF16, ctx) for s in range(UNROLL)]
            q_win = [sb(f"q_win{k}", [P, PLANES * H], BF16, ctx) for k in range(2)]
            ef = [sb(f"ef{k}", [P, W], F32, ctx) for k in range(2)]
            hot = [sb(f"hot_d{k}", [P, GROUP, P], BF16, ctx) for k in range(2)]
            hot_t = sb("hot_t_d", [P, W], BF16, ctx)
            hot_f = [sb(f"hot_f{k}", [P, GROUP, P], F32, ctx) for k in range(2)]
            h1 = sb("h1", [H, 2, WH], F32, ctx)
            h2 = sb("h2", [P, GROUP, H], F32, ctx)
            x_dst = sb("x_dst_d", [P, GROUP], F32, ctx)
            x_hot = sb("x_hot_d", [P, GROUP, P], BF16, ctx)
            x_hot_t = sb("x_hot_t_d", [P, W], BF16, ctx)
            x_hot_f = sb("x_hot_f", [P, GROUP, P], F32, ctx)
            x_q = sb("x_q", [P, PLANES * H], BF16, ctx)
            t_ps = ps("t_ps_d", [P, W], BF16, ctx)
            z1 = [ps(f"z1_{k}", [H, 512], F32, ctx) for k in range(2)]
            z2 = [ps(f"z2_{k}", [P, 4, H], F32, ctx) for k in range(2)]
            seg_ps = ps("seg_ps", [H, P], F32, ctx)
            x_t_ps = ps("x_t_ps_d", [P, W], BF16, ctx)
            x_seg_ps = ps("x_seg_ps", [H, P], F32, ctx)

            ef_zero = sem("ef_zero", ctx)
            ef_loaded = [sem(f"ef_loaded{k}", ctx) for k in range(2)]
            q_loaded = [sem(f"q_loaded{k}", ctx) for k in range(2)]
            idx_loaded = [sem(f"idx_loaded{s}", ctx) for s in range(UNROLL)]
            gathered = [sem(f"gathered{s}", ctx) for s in range(UNROLL)]
            hot_ready = sem("hot_ready_d", ctx)
            hot_f_ready = sem("hot_f_ready", ctx)
            t_made = sem("t_made_d", ctx)
            hot_t_ready = sem("hot_t_ready_d", ctx)
            z1_made = sem("z1_made", ctx)
            h1_ready = sem("h1_ready", ctx)
            z2_made = sem("z2_made", ctx)
            h2_ready = sem("h2_ready", ctx)
            seg_made = sem("seg_made", ctx)
            seg_added = sem("seg_added", ctx)
            acc_zero = sem("acc_zero", ctx)
            sp_turns = sem("sp_turns_d", ctx)
            pool_turns = sem("pool_turns_d", ctx)
            pe_turns = sem("pe_turns_d", ctx)
            x_dst_ready = sem("x_dst_ready_d", ctx)
            x_hot_ready = sem("x_hot_ready_d", ctx)
            x_t_made = sem("x_t_made_d", ctx)
            x_hot_t_ready = sem("x_hot_t_ready_d", ctx)
            x_loaded = sem("x_loaded_d", ctx)
            x_used = sem("x_used_d", ctx)
            x_dst_again = sem("x_dst_again", ctx)
            x_hot_f_ready = sem("x_hot_f_ready", ctx)
            x_seg_made = sem("x_seg_made", ctx)
            x_seg_added = sem("x_seg_added", ctx)
            block = ctx.enter_context(nc.Block())

            @block.sync
            def _(sp):
                def load_idx(q, s):
                    sp.dma_start(idx[s][:, :], src_col[:, bass.ds(q * GROUP, GROUP)]).then_inc(idx_loaded[s], 16)

                load_idx(0, 0)
                load_idx(1, 1)
                sp.wait_ge(ef_zero, 1)

                def step(q, s):
                    wait_past(sp, z1_made, q * 2 - 2)
                    sp.sem_inc(sp_turns, 1)
                    if not isinstance(q, int) or q + 2 < NG:
                        load_idx(q + 2, (s + 2) % UNROLL)
                    k = s % 2
                    sp.dma_start(ef[k][0:EF, :], edge_t[:, bass.ds(q * W, W)]).then_inc(ef_loaded[k], 16)
                    base = load_base(sp, q)
                    sp.dma_start(q_win[k][:, :], q_tab[bass.ds(base, P), :]).then_inc(q_loaded[k], 16)

                    def more(e, first, x):
                        sp.wait_ge(x_used, e + 1)
                        sp.sem_inc(sp_turns, 1)
                        sp.dma_start(x_q[:, :], q_tab[bass.ds(first, P), :]).then_inc(x_loaded, 16)
                    each_extra(sp, q, more)

                paced(sp, NG, step)

            @block.gpsimd
            def _(pool):
                pool.memset(ef[0][:, :], 0.0)
                pool.memset(ef[1][:, :], 0.0).then_inc(ef_zero, 1)

                def step(q, s):
                    pool.wait_ge(idx_loaded[s], in_slot(q, s, UNROLL, 16))
                    pool.sem_inc(pool_turns, 1)
                    wait_past(pool, z1_made, (q - UNROLL + 1) * 2)
                    pool.sem_inc(pool_turns, 1)
                    for j in range(GROUP):
                        pool.indirect_dma_start(p_got[s][:, j, :], None, p_tab,
                                                bass.IndirectOffsetOnAxis(idx[s][:, j:j + 1], 0)
                                                ).then_inc(gathered[s], 16)

                paced(pool, NG, step)

            @block.scalar
            def _(act):
                def step(q, s):
                    act.wait_ge(t_made, q + 1)
                    wait_past(act, z1_made, q * 2)
                    act.copy(hot_t[:, :], t_ps[:, :]).then_inc(hot_t_ready, 1)

                    def more(e, first, x):
                        act.wait_ge(x_t_made, e + 1)
                        act.copy(x_hot_t[:, :], x_t_ps[:, :]).then_inc(x_hot_t_ready, 1)
                    each_extra(act, q, more)
                    for k in range(2):
                        act.wait_ge(z1_made, q * 2 + (k + 1))
                        wait_past(act, z2_made, q * 2)
                        act.activation(h1[:, k, :], z1[k][:, 0:WH], ACT.Relu, bias=b1_col[:, 0:1]
                                       ).then_inc(h1_ready, 1)

                paced(act, NG, step)

            @block.tensor
            def _(pe):
                def second(q):
                    for k in range(2):
                        pe.wait_ge(h1_ready, q * 2 + (k + 1))
                        wait_past(pe, h2_ready, q * 2 - 1 + k)
                        for j in range(2):
                            last = pe.matmul(z2[k][:, j, :], h1[:, k, j * P:(j + 1) * P], w2_sb[:, :],
                                             start=True, stop=True)
                        last.then_inc(z2_made, 1)

                def into_nodes(out_ps, hots):
                    for j in range(GROUP):
                        last = pe.matmul(out_ps[:, :], h2[:, j, :], hots[:, j, :], start=(j == 0),
                                         stop=(j == GROUP - 1))
                    return last

                def segment(q, s):
                    pe.wait_ge(h2_ready, q * 2 + 2)
                    pe.wait_ge(hot_f_ready, q + 1)
                    wait_past(pe, seg_added, q)
                    into_nodes(seg_ps, hot_f[s % 2]).then_inc(seg_made, 1)

                    def more(e, first, x):
                        pe.wait_ge(x_hot_f_ready, e + 1)
                        into_nodes(x_seg_ps, x_hot_f).then_inc(x_seg_made, 1)
                    each_extra(pe, q, more)

                pe.sem_inc(x_used, 1)

                def step(q, s):
                    k2 = s % 2
                    pe.wait_ge(hot_ready, q + 1)
                    pe.sem_inc(pe_turns, 1)
                    wait_past(pe, hot_t_ready, q)
                    pe.sem_inc(pe_turns, 1)
                    for j in range(GROUP):
                        last = pe.transpose(t_ps[:, j * P:(j + 1) * P], hot[k2][:, j, :], ident_b[:, :])
                    last.then_inc(t_made, 1)
                    wait_past(pe, h1_ready, q * 2)
                    pe.wait_ge(ef_loaded[k2], in_slot(q, s, 2, 16))
                    for k in range(2):
                        pe.matmul(z1[k][:, 0:WH], w1c_sb[:, :], ef[k2][:, k * WH:(k + 1) * WH], start=True, stop=False,
                                  skip_group_check=True)
                    if not isinstance(q, int) or q > 0:
                        second(q - 1)
                    pe.wait_ge(gathered[s], in_slot(q, s, UNROLL, 16 * GROUP))
                    for j in range(GROUP):
                        for m in range(PLANES):
                            pe.matmul(z1[j // 2][:, (j % 2) * P:(j % 2 + 1) * P], p_got[s][:, j, m * H:(m + 1) * H],
                                      ident_b[:, :], start=False, stop=False, skip_group_check=True)

                    def add_q(k, planes, hots):
                        for m in range(PLANES):
                            last = pe.matmul(z1[k][:, 0:WH], planes[:, m * H:(m + 1) * H],
                                             hots[:, k * WH:(k + 1) * WH], start=False, stop=(m == PLANES - 1),
                                             skip_group_check=True)
                        return last

                    def more(e, first, x):
                        pe.wait_ge(x_hot_ready, e + 1)
                        pe.sem_inc(pe_turns, 1)
                        for j in range(GROUP):
                            last = pe.transpose(x_t_ps[:, j * P:(j + 1) * P], x_hot[:, j, :], ident_b[:, :])
                        last.then_inc(x_t_made, 1)
                        pe.wait_ge(x_hot_t_ready, e + 1)
                        pe.wait_ge(x_loaded, e * 16 + 16)
                        add_q(0, x_q, x_hot_t)
                        add_q(1, x_q, x_hot_t).then_inc(x_used, 1)
                    each_extra(pe, q, more)
                    pe.wait_ge(hot_t_ready, q + 1)
                    pe.wait_ge(q_loaded[k2], in_slot(q, s, 2, 16))
                    for k in range(2):
                        add_q(k, q_win[k2], hot_t).then_inc(z1_made, 1)
                    if not isinstance(q, int) or q > 0:
                        segment(q - 1, s - 1)

                paced(pe, NG, step)
                second(NG - 1)
                segment(NG - 1, UNROLL - 1)

            @block.vector
            def _(dve):
                dve.memset(seg_acc[:, :], 0.0).then_inc(acc_zero, 1)
                dve.wait_ge(acc_zero, 1)
                one_hots(dve, hot[0], 0).then_inc(hot_ready, 1)

                def shifted_dst(q, x, ready, e):
                    dve.tensor_scalar(x_dst[:, :], dst_f[:, bass.ds(q * GROUP, GROUP)],
                                      block_base[:, bass.ds(x + 1, 1)], None, ALU.subtract).then_inc(ready, 1)
                    dve.wait_ge(ready, e + 1)

                def add_seg(first, a):
                    at = seg_acc[:, bass.ds(first, P)]
                    return dve.tensor_tensor(at, at, a[:, :], ALU.add)

                def make_h2(q):
                    for k in range(2):
                        dve.wait_ge(z2_made, q * 2 + (k + 1))
                        dve.tensor_tensor(h2[:, 2 * k:2 * k + 2, :], z2[k][:, 0:2, :],
                                          nb2[:, :].unsqueeze(1).to_broadcast([P, 2, H]), ALU.max
                                          ).then_inc(h2_ready, 1)

                def add_segments(q):
                    dve.wait_ge(seg_made, q + 1)
                    wait_past(dve, seg_added, q)
                    add_seg(load_base(dve, q), seg_ps).then_inc(seg_added, 1)

                    def more(e, first, x):
                        shifted_dst(q, x, x_dst_again, e)
                        one_hots(dve, x_hot_f, q, x_dst).then_inc(x_hot_f_ready, 1)
                        dve.wait_ge(seg_added, q + 1)
                        dve.wait_ge(x_seg_made, e + 1)
                        add_seg(first, x_seg_ps).then_inc(x_seg_added, 1)
                        dve.wait_ge(x_seg_added, e + 1)
                    each_extra(dve, q, more)

                def step(q, s):
                    k = s % 2
                    if not isinstance(q, int) or q + 1 < NG:
                        wait_past(dve, t_made, q)
                        one_hots(dve, hot[1 - k], q + 1).then_inc(hot_ready, 1)
                    if not isinstance(q, int) or q > 0:
                        make_h2(q - 1)
                    wait_past(dve, seg_made, q - 1)
                    one_hots(dve, hot_f[k], q).then_inc(hot_f_ready, 1)

                    def more(e, first, x):
                        shifted_dst(q, x, x_dst_ready, e)
                        one_hots(dve, x_hot, q, x_dst).then_inc(x_hot_ready, 1)
                        dve.wait_ge(x_t_made, e + 1)
                    each_extra(dve, q, more)
                    if not isinstance(q, int) or q > 0:
                        add_segments(q - 1)

                paced(dve, NG, step)
                make_h2(NG - 1)
                add_segments(NG - 1)

        with ExitStack() as ctx:
            inv = sb("inv", [P, NB], F32, ctx)
            seg = [sb(f"seg{k}", [H, CB * P], F32, ctx) for k in range(2)]
            scratch = sb("scratch_e", [P, NB, F], F32, ctx)
            m_ps = [ps(f"m_ps{k}", [P, CB, F], F32, ctx) for k in range(2)]
            chain = sem("chain_e", ctx)
            seg_ready = sem("seg_ready", ctx)
            m_made = sem("m_made", ctx)
            added = sem("added", ctx)
            base_ready = sem("base_ready", ctx)
            stored = sem("stored", ctx)
            block = ctx.enter_context(nc.Block())

            @block.scalar
            def _(act):
                for n in range(NK):
                    wait_past(act, m_made, n - 1)
                    act.copy(seg[n % 2][:, :], seg_acc[:, n * CB * P:(n + 1) * CB * P]).then_inc(seg_ready, 1)

            @block.tensor
            def _(pe):
                for n in range(NK):
                    pe.wait_ge(seg_ready, n + 1)
                    wait_past(pe, added, n - 1)
                    for c in range(CB):
                        last = pe.matmul(m_ps[n % 2][:, c, :], seg[n % 2][:, c * P:(c + 1) * P], w3_sb[:, :],
                                         start=True, stop=True)
                    last.then_inc(m_made, 1)

            @block.vector
            def _(dve):
                link = linker(dve, chain)
                full = [P, NB, F]
                link(dve.tensor_tensor(x1[:, :, :], x1[:, :, :], act_in[:, :, :], ALU.add))
                link(dve.tensor_scalar(inv[:, :], dst_cnt[:, :], 1.0, None, ALU.max))
                link(dve.reciprocal(inv[:, :], inv[:, :]))
                link(dve.tensor_tensor(scratch[:, :, :], dst_cnt[:, :].unsqueeze(2).to_broadcast(full),
                                       c_bc[:, :].unsqueeze(1).to_broadcast(full), ALU.mult))
                for n in range(NK):
                    part = slice(n * CB, (n + 1) * CB)
                    dve.wait_ge(m_made, n + 1)
                    link(dve.tensor_tensor(scratch[:, part, :], scratch[:, part, :], m_ps[n % 2][:, :, :], ALU.add))
                    link(dve.tensor_tensor(scratch[:, part, :], scratch[:, part, :],
                                           inv[:, part].unsqueeze(2).to_broadcast([P, CB, F]), ALU.mult))
                    dve.tensor_tensor(x1[:, part, :], x1[:, part, :], scratch[:, part, :], ALU.add
                                      ).then_inc(added, 1)

            @block.sync
            def _(sp):
                stores = 0
                for n in range(NK):
                    low, high = n * CB, (n + 1) * CB
                    whole_blocks = min(high, N // P)
                    sp.wait_ge(added, n + 1)
                    if whole_blocks > low:
                        stores += 1
                        sp.dma_start(out[low * P:whole_blocks * P, :].rearrange("(b p) f -> p b f", p=P),
                                     x1[:, low:whole_blocks, :]).then_inc(stored, 16)
                    if high * P > N:
                        stores += 1
                        sp.dma_start(out[whole_blocks * P:N, :], x1[0:N % P, whole_blocks, :]).then_inc(stored, 16)
                sp.wait_ge(stored, 16 * stores)


def layout(x, src, dst, edge_attr_16, L0_gnn_W, L0_gnn_b, L1_gnn_W1, L1_gnn_b1, L1_gnn_W2, L1_gnn_b2, L1_gnn_W3,
           L1_gnn_b3):
    import numpy as np

    def a(v):
        return np.ascontiguousarray(v)

    n, f = x.shape
    e, ef = edge_attr_16.shape
    padded = GROUP * UNROLL * -(-e // (P * GROUP * UNROLL))
    more = padded * P - e
    h = L1_gnn_W2.shape[0]
    src_p = np.concatenate([src, np.full(more, n + -n % P, src.dtype)])
    dst_p = np.concatenate([dst, np.full(more, PAD_NODE, dst.dtype)])
    w1 = np.asarray(L1_gnn_W1)
    return {
        "x": a(np.concatenate([x, np.zeros((-n % P, f), x.dtype)])),
        "src_col": a(src_p.reshape(padded, P).T),
        "dst_col": a(dst_p.reshape(padded, P).T),
        "dst_row": a(dst_p.reshape(padded // GROUP, GROUP * P)),
        "edge_t": a(np.concatenate([edge_attr_16, np.zeros((more, ef), edge_attr_16.dtype)]).T),
        "w0_t": a(np.asarray(L0_gnn_W).T),
        "b0": a(np.asarray(L0_gnn_b).reshape(1, f)),
        "w1ab": a(np.concatenate([w1[0:f], w1[f:2 * f]], axis=1)),
        "w1c": a(w1[2 * f:]),
        "b1": a(np.asarray(L1_gnn_b1).reshape(h, 1)),
        "w2": a(L1_gnn_W2),
        "b2": a(np.asarray(L1_gnn_b2).reshape(1, h)),
        "w3": a(L1_gnn_W3),
        "b3": a(np.asarray(L1_gnn_b3).reshape(1, f)),
    }


def kernel(**inputs):
    import numpy as np
    import concourse.bacc as bacc
    from concourse.bass_utils import run_bass_kernel_spmd

    inputs = {k: np.asarray(v) for k, v in inputs.items()}
    nc = bacc.Bacc("TRN2", target_bir_lowering=False, num_devices=1)
    arrays = layout(**inputs)
    args = [nc.dram_tensor(f"in_{k}", v.shape, mybir.dt.from_np(v.dtype), kind="ExternalInput").ap()
            for k, v in arrays.items()]
    out = nc.dram_tensor("out_0", inputs["x"].shape, F32, kind="ExternalOutput").ap()
    build_gnn(nc, *args, out)
    r = run_bass_kernel_spmd(nc, [{f"in_{k}": v for k, v in arrays.items()}], core_ids=[0])
    return r.results[0]["out_0"]
```

```python
from contextlib import ExitStack

import concourse.bass as bass
from concourse import mybir

P = 128
GROUP = 4
UNROLL = 4
TABLES = GROUP
PLANES = 3
PAD_NODE = 1 << 20
EPS = 1e-5

ALU = mybir.AluOpType
ACT = mybir.ActivationFunctionType
AX = mybir.AxisListType
F32 = mybir.dt.float32
BF16 = mybir.dt.bfloat16
I32 = mybir.dt.int32


def divisor(n, most):
    return max(d for d in range(1, most + 1) if n % d == 0)


def paced(eng, steps, body):
    for s in range(UNROLL):
        body(s, s)
    with eng.Fori(1, steps // UNROLL - 1) as r:
        for s in range(UNROLL):
            body(eng.snap(r * UNROLL + s), s)
    for s in range(UNROLL):
        body(steps - UNROLL + s, s)


def wait_past(eng, sem, value):
    if not isinstance(value, int) or value > 0:
        eng.wait_ge(sem, value)


def lagged(eng, steps, lag, body):
    head = lag + lag % 2
    pairs = max(0, steps - head) // 2
    for k in range(head):
        body(k, k % 2)
    if pairs:
        with eng.Fori(head // 2, head // 2 + pairs) as r:
            for s in range(2):
                body(eng.snap(r * 2 + s), s)
    for k in range(head + 2 * pairs, steps + lag):
        body(k, k % 2)


def in_slot(q, slot, slots, per):
    return (q - slot) * (per // slots) + (slot // slots + 1) * per


def build_gnn(nc, x, src_col, dst_col, dst_row, edge_t, w0_t, b0, w1ab, w1c, b1, w2, b2, w3, b3, out):
    N, F = out.shape
    NB = x.shape[0] // P
    NP = NB * P
    NPP = NP + P
    TP = src_col.shape[1]
    NG = TP // GROUP
    W = GROUP * P
    WH = W // 2
    EF = edge_t.shape[0]
    H = w2.shape[0]
    CB = divisor(NB, 7)
    NK = NB // CB
    HG = divisor(NG, 7)
    CHUNKS = NG // HG
    PARTS = [(NB * n // 4, NB * (n + 1) // 4) for n in range(4)]
    SCANS = (NG - 1).bit_length()
    GP = divisor(NG, P)
    GK = NG // GP
    assert NG % UNROLL == 0 and NG >= 3 * UNROLL and H == P

    def dram(name, shape, dt):
        return nc.dram_tensor(name, shape, dt).ap()

    sum_tab = [dram(f"sum_tab{j}", [NPP, F], F32) for j in range(TABLES)]
    g_tab = dram("g_tab", [NPP, PLANES * F], BF16)
    p_tab = dram("p_tab", [NPP, PLANES * H], BF16)
    q_tab = dram("q_tab", [NPP, PLANES * H], BF16)
    ext_tab = dram("ext_tab", [2, NG], F32)
    cnt_tab = dram("cnt_tab", [1, NPP], F32)

    def node_view(table):
        return table[0:NP, :].rearrange("(b p) f -> p b f", p=P)

    with ExitStack() as whole:
        def sb(name, shape, dt, ctx=whole):
            return ctx.enter_context(nc.sbuf_tensor(name, shape, dt))

        def ps(name, shape, dt, ctx):
            return ctx.enter_context(nc.psum_tensor(name, shape, dt))

        def sem(name, ctx=whole):
            return ctx.enter_context(nc.semaphore(name))

        src_f = sb("src_f", [P, TP], F32)
        dst_rel = sb("dst_rel", [P, TP], F32)
        lo_b = sb("lo_b", [P, TP], BF16)
        hi_b = sb("hi_b", [P, TP], BF16)
        x1 = sb("x1", [P, NB, F], F32)
        act_in = sb("act_in", [P, NB, F], F32)
        sched = sb("sched", [1, 3, NG], I32)
        extra_total = sb("extra_total", [1, 1], I32)
        block_base = sb("block_base", [P, NB + 1], F32)
        iota_b = sb("iota_b", [P, P], BF16)
        ident_f = sb("ident_f", [P, P], F32)
        ident_b = sb("ident_b", [P, P], BF16)
        ident_hi = sb("ident_hi", [P, P], BF16)
        ones_b = sb("ones_b", [P, 1], BF16)
        zero_b = sb("zero_b", [P, PLANES * H], BF16)
        below = sb("below", [P, P], F32)
        trash = sb("trash", [P, 1], F32)
        deg_is = sb("deg_is", [P, NB], F32)
        half = sb("half", [P, NB], F32)
        stat = sb("stat", [P, NB], F32)

        def linker(eng, chain):
            count = [0]

            def link(ins):
                count[0] += 1
                ins.then_inc(chain, 1)
                eng.wait_ge(chain, count[0])
            return link

        def center(dve, link, a, out_a, squares, st):
            nodes = [P, a.shape[1], F]
            link(dve.tensor_reduce(st, a, AX.X, ALU.add))
            link(dve.tensor_scalar(st, st, 1.0 / F, None, ALU.mult))
            link(dve.tensor_tensor(out_a, a, st.unsqueeze(2).to_broadcast(nodes), ALU.subtract))
            link(dve.tensor_tensor(squares, out_a, out_a, ALU.mult))
            link(dve.tensor_reduce(st, squares, AX.X, ALU.add))
            link(dve.tensor_scalar(st, st, 1.0 / F, EPS, ALU.mult, ALU.add))

        def load_base(eng, q):
            return eng.value_load(sched[0:1, 0, bass.ds(q, 1)], min_val=0, max_val=NP - P)

        def each_extra(eng, body):
            total = eng.value_load(extra_total[0:1, 0:1], min_val=0, max_val=NB * NG)
            with eng.If(total > 0):
                with eng.Fori(0, NG) as q:
                    extra = eng.value_load(sched[0:1, 1, bass.ds(q, 1)], min_val=0, max_val=NB)
                    with eng.If(extra > 0):
                        before = eng.value_load(sched[0:1, 2, bass.ds(q, 1)], min_val=0, max_val=NB * NG)
                        base = load_base(eng, q)
                        with eng.Fori(0, extra) as x:
                            first = eng.snap(nc.s_assert_within(base + (x + 1) * P, 0, NP))
                            body(eng.snap(before + x), q, first, x)

        def one_hots(dve, hot, dst):
            return dve.tensor_tensor(hot[:, :, :], iota_b[:, :].unsqueeze(1).to_broadcast([P, GROUP, P]),
                                     dst.unsqueeze(2).to_broadcast([P, GROUP, P]), ALU.is_equal)

        def in_group(table, q):
            return table[:, bass.ds(q * GROUP, GROUP)]

        def each_tile(a):
            return [a[:, j * P:(j + 1) * P] for j in range(GROUP)]

        def transpose_hots(pe, out_ps, hot):
            for j, out_tile in enumerate(each_tile(out_ps)):
                last = pe.transpose(out_tile, hot[:, j, :], ident_b[:, :])
            return last

        with ExitStack() as ctx:
            src_i = sb("src_i", [P, TP], I32, ctx)
            dst_i = sb("dst_i", [P, TP], I32, ctx)
            hot_lo = [sb(f"hot_lo{k}", [P, HG, P, GROUP], BF16, ctx) for k in range(2)]
            hot_hi = [sb(f"hot_hi{k}", [P, HG, NB, GROUP], BF16, ctx) for k in range(2)]
            digits = sb("digits", [P, P, GROUP], BF16, ctx)
            scratch = sb("scratch", [P, NB, F], F32, ctx)
            late = sb("late", [P, max(NB * PLANES * F, 2 * GK * W)], BF16, ctx)
            g_planes = late[:, 0:NB * PLANES * F].rearrange("p (b f) -> p b f", b=NB)
            squares = late[:, 0:NB * F * 2].bitcast(F32).rearrange("p (b f) -> p b f", b=NB)
            row_view = late[0:GP, 0:2 * GK * W].bitcast(I32).rearrange("p (k e) -> p k e", k=GK)
            base_col = sb("base_col", [P, NG], F32, ctx)
            ext = sb("ext", [GP, 2, GK], F32, ctx)
            ext_bc = sb("ext_bc", [P, 2, NG], F32, ctx)
            scan = [sb(f"scan{k}", [1, NG], F32, ctx) for k in range(2)]
            extra_i = sb("extra_i", [1, NG], I32, ctx)
            extra_f = sb("extra_f", [1, NG], F32, ctx)
            hist = ps("hist", [P, NB], F32, ctx)

            loaded = sem("loaded", ctx)
            x_loaded = sem("x_loaded", ctx)
            row_loaded = sem("row_loaded", ctx)
            const_ready = sem("const_ready", ctx)
            hot_ready = sem("hot_ready", ctx)
            hot_used = sem("hot_used", ctx)
            ext_ready = sem("ext_ready", ctx)
            ext_saved = sem("ext_saved", ctx)
            ext_loaded = sem("ext_loaded", ctx)
            zero_ready = sem("zero_ready", ctx)
            zeroed = sem("zeroed", ctx)
            g_ready = sem("g_ready", ctx)
            g_saved = sem("g_saved", ctx)
            ids_copied = sem("ids_copied", ctx)
            digits_ready = sem("digits_ready", ctx)
            digits_copied = sem("digits_copied", ctx)
            extra_ready = sem("extra_ready", ctx)
            scan_ready = sem("scan_ready", ctx)
            pow_ask = sem("pow_ask", ctx)
            pow_done = sem("pow_done", ctx)
            chain = sem("chain", ctx)
            pool_chain = sem("pool_chain", ctx)
            block = ctx.enter_context(nc.Block())

            @block.sync
            def _(sp):
                sp.dma_start(row_view, dst_row.rearrange("(p k) e -> p k e", k=GK)).then_inc(row_loaded, 16)
                sp.dma_start(src_i[:, :], src_col).then_inc(loaded, 16)
                sp.dma_start(dst_i[:, :], dst_col).then_inc(loaded, 16)
                sp.dma_start(x1[:, :, :], x.rearrange("(b p) f -> p b f", p=P)).then_inc(x_loaded, 16)
                sp.wait_ge(ext_ready, 1)
                for k in range(2):
                    sp.dma_start(ext_tab[k:k + 1, :].rearrange("o (p k) -> p (o k)", k=GK),
                                 ext[:, k, :]).then_inc(ext_saved, 16)
                sp.wait_ge(ext_saved, 32)
                sp.dma_start(ext_bc[:, :, :], ext_tab.unsqueeze(0).to_broadcast([P, 2, NG])).then_inc(ext_loaded, 16)
                sp.wait_ge(const_ready, 1)
                sp.dma_start(g_tab[NP:NPP, :], zero_b[:, 0:PLANES * F]).then_inc(g_saved, 16)
                sp.dma_start(q_tab[NP:NPP, :], zero_b[:, :]).then_inc(g_saved, 16)
                sp.dma_start(p_tab[NP:NPP, :], zero_b[:, :]).then_inc(g_saved, 16)
                for n, (a, z) in enumerate(PARTS):
                    sp.wait_ge(g_ready, n + 1)
                    sp.dma_start(node_view(g_tab)[:, a:z, :], g_planes[:, a:z, :]).then_inc(g_saved, 16)
                sp.wait_ge(g_saved, 48 + 16 * len(PARTS))

            @block.scalar
            def _(act):
                act.wait_ge(loaded, 32)
                act.copy(src_f[:, :], src_i[:, :])
                act.copy(dst_rel[:, :], dst_i[:, :]).then_inc(ids_copied, 1)
                act.wait_ge(digits_ready, 1)
                act.copy(lo_b[:, :], dst_i[:, :])
                act.copy(hi_b[:, :], src_i[:, :]).then_inc(digits_copied, 1)
                act.wait_ge(zero_ready, 1)
                act.wait_ge(ext_loaded, 16)
                for j in range(TABLES):
                    act.dma_start(node_view(sum_tab[j]), scratch[:, :, :]).then_inc(zeroed, 16)
                    act.dma_start(sum_tab[j][NP:NPP, :], scratch[:, 0, :]).then_inc(zeroed, 16)
                act.dma_start(cnt_tab.rearrange("o (b p) -> (o b) p", p=P),
                              scratch[0:NB + 1, :, :].rearrange("p b f -> p (b f)")[:, 0:P]).then_inc(zeroed, 16)
                act.wait_ge(zeroed, 32 * TABLES + 16)

            @block.gpsimd
            def _(pool):
                link = linker(pool, pool_chain)
                pool.memset(scratch[:, :, :], 0.0).then_inc(zero_ready, 1)

                def iota(dst, steps, base, by_partition):
                    return pool.iota(dst, steps, base=base, channel_multiplier=by_partition,
                                     allow_small_or_imprecise_dtypes=True)

                iota(iota_b[:, :], [[1, P]], 0, 0)
                iota(digits[:, :, :], [[1, P], [0, GROUP]], 0, 0)
                iota(block_base[:, :], [[P, NB + 1]], 0, 0)
                iota(trash[:, :], [[0, 1]], NP, 1)
                pool.memset(half[:, :], -0.5)
                pool.memset(ones_b[:, :], 1.0)
                pool.memset(zero_b[:, :], 0.0)
                for m in (ident_f, below):
                    link(pool.memset(m[:, :], 0.0))
                link(pool.affine_select(ident_f[:, :], ident_f[:, :], [[-1, P]], ALU.not_equal, 1.0,
                                        base=0, channel_multiplier=1))
                link(pool.affine_select(below[:, :], below[:, :], [[1, P]], ALU.is_ge, 1.0,
                                        base=0, channel_multiplier=-1))
                link(pool.tensor_copy(ident_b[:, :], ident_f[:, :]))
                pool.tensor_scalar(ident_hi[:, :], ident_f[:, :], float(P), None, ALU.mult).then_inc(const_ready, 1)
                pool.wait_ge(pow_ask, 1)
                link(pool.tensor_tensor(stat[:, :], stat[:, :], half[:, :], ALU.pow))
                link(pool.tensor_tensor(act_in[:, :, :], act_in[:, :, :],
                                        stat[:, :].unsqueeze(2).to_broadcast([P, NB, F]), ALU.mult))
                link(pool.tensor_scalar(act_in[:, :, :], act_in[:, :, :], 0.0, None, ALU.max))
                pool.wait_ge(extra_ready, 1)
                for n in range(SCANS):
                    old, new, d = scan[n % 2], scan[1 - n % 2], 1 << n
                    link(pool.tensor_tensor(new[:, d:], old[:, d:], old[:, 0:NG - d], ALU.add))
                    link(pool.tensor_copy(new[:, 0:d], old[:, 0:d]))
                by_group = dst_rel[:, :].rearrange("p (g j) -> p g j", j=GROUP)
                pool.tensor_tensor(by_group, by_group, base_col[:, :].unsqueeze(2).to_broadcast([P, NG, GROUP]),
                                   ALU.subtract).then_inc(scan_ready, 1)
                for n, (a, z) in enumerate(PARTS):
                    pool.wait_ge(pow_ask, n + 2)
                    pool.tensor_tensor(deg_is[:, a:z], deg_is[:, a:z], half[:, a:z], ALU.pow).then_inc(pow_done, 1)

            @block.tensor
            def _(pe):
                def count_chunk(n, k):
                    pe.wait_ge(hot_ready, n + 1)
                    for c in range(HG):
                        for j in range(GROUP):
                            last = pe.matmul(hist[:, :], hot_lo[k][:, c, :, j], hot_hi[k][:, c, :, j],
                                             start=False, stop=False, skip_group_check=True)
                    last.then_inc(hot_used, 1)

                pe.wait_ge(const_ready, 1)
                pe.matmul(hist[:, :], zero_b[:, 0:P], zero_b[:, 0:NB], start=True, stop=False, skip_group_check=True)
                pe.sem_inc(hot_used, 2)
                with pe.Fori(0, CHUNKS // 2) as r:
                    count_chunk(r * 2, 0)
                    count_chunk(r * 2 + 1, 1)
                if CHUNKS % 2:
                    count_chunk(CHUNKS - 1, 0)

            @block.vector
            def _(dve):
                link = linker(dve, chain)
                dve.wait_ge(row_loaded, 16)
                dve.tensor_reduce(ext[:, 0, :], row_view, AX.X, ALU.min)
                dve.tensor_reduce(ext[:, 1, :], row_view, AX.X, ALU.max).then_inc(ext_ready, 1)

                dve.wait_ge(loaded, 32)
                dve.wait_ge(ids_copied, 1)
                link(dve.tensor_scalar(dst_i[:, :], src_i[:, :], P - 1, None, ALU.bitwise_and))
                dve.tensor_scalar(src_i[:, :], src_i[:, :], P.bit_length() - 1, None, ALU.logical_shift_right
                                  ).then_inc(digits_ready, 1)

                dve.wait_ge(x_loaded, 16)
                dve.wait_ge(ext_ready, 1)
                center(dve, link, x1[:, :, :], act_in[:, :, :], squares, stat[:, :])
                dve.sem_inc(pow_ask, 1)

                dve.wait_ge(ext_loaded, 16)
                link(dve.tensor_scalar(base_col[:, :], ext_bc[:, 0, :], float(NP - P), None, ALU.min))
                link(dve.tensor_copy(sched[:, 0, :], base_col[0:1, :]))
                link(dve.scalar_tensor_tensor(extra_i[:, :], ext_bc[0:1, 1, :], float(N - 1), base_col[0:1, :],
                                              ALU.min, ALU.subtract))
                link(dve.tensor_scalar(sched[:, 1, :], extra_i[:, :], P.bit_length() - 1, None,
                                       ALU.logical_shift_right))
                link(dve.tensor_copy(extra_f[:, :], sched[:, 1, :]))
                dve.tensor_copy(scan[0][:, :], sched[:, 1, :]).then_inc(extra_ready, 1)

                def hot_chunk(n, k):
                    dve.wait_ge(hot_used, n + 1)
                    for hots, digit, width in ((hot_lo[k], lo_b, P), (hot_hi[k], hi_b, NB)):
                        shape = [P, HG, width, GROUP]
                        tiles = digit[:, bass.ds(n * HG * GROUP, HG * GROUP)].rearrange("p (g j) -> p g j", j=GROUP)
                        values = digits[:, 0:width, :].unsqueeze(1).to_broadcast(shape)
                        last = dve.tensor_tensor(hots[:, :, :, :], values, tiles.unsqueeze(2).to_broadcast(shape),
                                                 ALU.is_equal)
                    last.then_inc(hot_ready, 1)

                dve.wait_ge(const_ready, 1)
                dve.wait_ge(digits_copied, 1)
                with dve.Fori(0, CHUNKS // 2) as r:
                    hot_chunk(r * 2, 0)
                    hot_chunk(r * 2 + 1, 1)
                if CHUNKS % 2:
                    hot_chunk(CHUNKS - 1, 0)

                dve.wait_ge(hot_used, CHUNKS + 2)
                dve.wait_ge(scan_ready, 1)
                dve.wait_ge(zeroed, 32 * TABLES + 16)
                for a, z in PARTS:
                    dve.tensor_scalar(deg_is[:, a:z], hist[:, a:z], 1.0, None, ALU.max).then_inc(pow_ask, 1)
                scanned = scan[SCANS % 2]
                link(dve.tensor_tensor(sched[:, 2, :], scanned[:, :], extra_f[:, :], ALU.subtract))
                link(dve.tensor_copy(extra_total[:, :], scanned[:, NG - 1:NG]))
                for n, (a, z) in enumerate(PARTS):
                    dve.wait_ge(pow_done, n + 1)
                    link(dve.scalar_tensor_tensor(deg_is[:, a:z], hist[:, a:z], 0.0, deg_is[:, a:z], ALU.is_gt,
                                                  ALU.mult))
                    part = scratch[:, a:z, :]
                    link(dve.tensor_tensor(part, act_in[:, a:z, :],
                                           deg_is[:, a:z].unsqueeze(2).to_broadcast([P, z - a, F]), ALU.mult))
                    for m in range(PLANES):
                        plane = g_planes[:, a:z, m * F:(m + 1) * F]
                        link(dve.tensor_copy(plane, part))
                        if m < PLANES - 1:
                            link(dve.tensor_tensor(part, part, plane, ALU.subtract))
                    dve.sem_inc(g_ready, 1)

        def src_along_rows(pe, src_ps, q):
            for j, out_tile in enumerate(each_tile(src_ps)):
                t = bass.ds(q * GROUP + j, 1)
                pe.matmul(out_tile, hi_b[:, t].to_broadcast([P, P]), ident_hi[:, :], start=True, stop=False)
                last = pe.matmul(out_tile, lo_b[:, t].to_broadcast([P, P]), ident_b[:, :], start=False, stop=True)
            return last

        def count_by_node(pe, cnt_ps, hot):
            for j in range(GROUP):
                last = pe.matmul(cnt_ps[:, :], ones_b[:, :], hot[:, j, :], start=(j == 0), stop=(j == GROUP - 1))
            return last

        def rows_by_dst(pe, rows_ps, hot_t, g_win):
            for j, hot_tile in enumerate(each_tile(hot_t)):
                for m in range(PLANES):
                    last = pe.matmul(rows_ps[:, j, :], hot_tile, g_win[:, m * F:(m + 1) * F],
                                     start=(m == 0), stop=(m == PLANES - 1))
            return last

        def sum_same(pe, comb_ps, same, rows):
            for j in range(GROUP):
                last = pe.matmul(comb_ps[:, j, :], same[:, j, :], rows[:, j, :], start=True, stop=True)
            return last

        def find_same(dve, same, src_ps, q):
            return dve.tensor_tensor(same[:, :, :], src_ps[:, :].rearrange("p (j e) -> p j e", j=GROUP),
                                     in_group(src_f, q).unsqueeze(2).to_broadcast([P, GROUP, P]), ALU.is_equal)

        def find_dup(dve, junk, same, dup):
            for j in range(GROUP):
                last = dve.tensor_tensor_reduce(junk[:, j, :], same[:, j, :], below[:, :], 1.0, 0.0, ALU.mult,
                                                ALU.max, dup[:, j:j + 1])
            return last

        def find_moved(dve, moved, dup, q):
            return dve.scalar_tensor_tensor(moved[:, :], in_group(src_f, q), trash[:, 0:1], dup[:, :],
                                            ALU.subtract, ALU.mult)

        def find_index(dve, idx, moved, q):
            return dve.tensor_tensor(idx[:, :], in_group(src_f, q), moved[:, :], ALU.subtract)

        def scatter(pool, j, idx, vals, landed):
            pool.indirect_dma_start(sum_tab[j], bass.IndirectOffsetOnAxis(idx[:, j:j + 1], 0), vals[:, j, :], None,
                                    compute_op=ALU.add).then_inc(landed[j], 16)

        def add_count(dve, cnt_acc, first, cnt_ps):
            at = cnt_acc[0:1, bass.ds(first, P)]
            return dve.tensor_tensor(at, at, cnt_ps[:, :], ALU.add)

        with ExitStack() as life:
            hot = [sb(f"hot{k}", [P, GROUP, P], BF16, life) for k in range(2)]
            hot_t = sb("hot_t", [P, W], BF16, life)
            g_win = [sb(f"g_win{k}", [P, PLANES * F], BF16, life) for k in range(2)]
            same = [sb(f"same{k}", [P, GROUP, P], F32, life) for k in range(2)]
            junk = sb("junk", [P, GROUP, P], F32, life)
            dup = sb("dup", [P, GROUP], F32, life)
            moved = sb("moved", [P, GROUP], F32, life)
            rows = sb("rows", [P, GROUP, F], F32, life)
            vals = [sb(f"vals{k}", [P, GROUP, F], F32, life) for k in range(2)]
            idx = [sb(f"idx{k}", [P, GROUP], I32, life) for k in range(2)]
            cnt_acc = sb("cnt_acc", [1, NPP], F32, life)
            x_dst = sb("x_dst", [P, GROUP], F32, life)
            t_ps = ps("t_ps", [P, W], BF16, life)
            cnt_ps = ps("cnt_ps", [1, P], F32, life)
            src_ps = ps("src_ps", [P, W], F32, life)
            rows_ps = ps("rows_ps", [P, GROUP, F], F32, life)
            comb_ps = ps("comb_ps", [P, GROUP, F], F32, life)

            with ExitStack() as ctx:
                hot_ready = sem("hot_ready_b", ctx)
                front_made = sem("front_made", ctx)
                hot_t_ready = sem("hot_t_ready", ctx)
                g_loaded = [sem(f"g_loaded{k}", ctx) for k in range(2)]
                rows_made = sem("rows_made", ctx)
                rows_kept = sem("rows_kept", ctx)
                same_ready = sem("same_ready", ctx)
                comb_made = sem("comb_made", ctx)
                vals_ready = sem("vals_ready", ctx)
                idx_ready = sem("idx_ready", ctx)
                cnt_added = sem("cnt_added", ctx)
                dup_steps = sem("dup_steps", ctx)
                cnt_zero = sem("cnt_zero", ctx)
                scattered = [sem(f"scattered{j}", ctx) for j in range(TABLES)]
                sp_turns = sem("sp_turns", ctx)
                pool_turns = sem("pool_turns", ctx)
                pe_turns = sem("pe_turns", ctx)
                dve_turns = sem("dve_turns", ctx)
                block = ctx.enter_context(nc.Block())
                STEPS = 2

                @block.sync
                def _(sp):
                    sp.dma_start(cnt_acc[:, :], cnt_tab).then_inc(cnt_zero, 16)

                    def step(q, s):
                        wait_past(sp, rows_made, q - 1)
                        sp.sem_inc(sp_turns, 1)
                        base = load_base(sp, q)
                        sp.dma_start(g_win[s % 2][:, :], g_tab[bass.ds(base, P), :]).then_inc(g_loaded[s % 2], 16)

                    paced(sp, NG, step)

                @block.scalar
                def _(act):
                    def keep_hot_t(q):
                        act.wait_ge(front_made, q + 1)
                        wait_past(act, rows_made, q)
                        act.copy(hot_t[:, :], t_ps[:, :]).then_inc(hot_t_ready, 1)

                    keep_hot_t(0)

                    def step(q, s):
                        act.wait_ge(rows_made, q + 1)
                        wait_past(act, comb_made, q)
                        act.copy(rows[:, :, :], rows_ps[:, :, :]).then_inc(rows_kept, 1)
                        if not isinstance(q, int) or q + 1 < NG:
                            keep_hot_t(q + 1)
                        act.wait_ge(comb_made, q + 1)
                        for j in range(TABLES):
                            wait_past(act, scattered[j], (q - 1) * 16)
                        act.copy(vals[s % 2][:, :, :], comb_ps[:, :, :]).then_inc(vals_ready, 1)

                    paced(act, NG, step)

                @block.tensor
                def _(pe):
                    def front(q, k):
                        pe.wait_ge(hot_ready, q + 1)
                        wait_past(pe, hot_t_ready, q)
                        pe.sem_inc(pe_turns, 1)
                        transpose_hots(pe, t_ps, hot[k])
                        wait_past(pe, cnt_added, q)
                        count_by_node(pe, cnt_ps, hot[k])
                        wait_past(pe, same_ready, q)
                        src_along_rows(pe, src_ps, q).then_inc(front_made, 1)

                    front(0, 0)

                    def step(q, s):
                        k = s % 2
                        wait_past(pe, rows_kept, q)
                        pe.wait_ge(hot_t_ready, q + 1)
                        pe.wait_ge(g_loaded[k], in_slot(q, s, 2, 16))
                        rows_by_dst(pe, rows_ps, hot_t, g_win[k]).then_inc(rows_made, 1)
                        if not isinstance(q, int) or q + 1 < NG:
                            front(q + 1, 1 - k)
                        pe.wait_ge(same_ready, q + 1)
                        pe.wait_ge(rows_kept, q + 1)
                        wait_past(pe, vals_ready, q)
                        sum_same(pe, comb_ps, same[k], rows).then_inc(comb_made, 1)

                    paced(pe, NG, step)

                @block.vector
                def _(dve):
                    dve.memset(junk[:, :, :], 0.0)
                    one_hots(dve, hot[0], in_group(dst_rel, 0)).then_inc(hot_ready, 1)

                    def step(q, s):
                        k = s % 2
                        if not isinstance(q, int) or q + 1 < NG:
                            wait_past(dve, front_made, q)
                            one_hots(dve, hot[1 - k], in_group(dst_rel, q + 1)).then_inc(hot_ready, 1)
                        wait_past(dve, comb_made, q - 1)
                        dve.wait_ge(front_made, q + 1)
                        find_same(dve, same[k], src_ps, q).then_inc(same_ready, 1)
                        wait_past(dve, cnt_added, q)
                        if isinstance(q, int) and q == 0:
                            dve.wait_ge(cnt_zero, 16)
                        add_count(dve, cnt_acc, load_base(dve, q), cnt_ps).then_inc(cnt_added, 1)
                        dve.wait_ge(same_ready, q + 1)
                        dve.sem_inc(dve_turns, 1)
                        find_dup(dve, junk, same[k], dup).then_inc(dup_steps, 1)
                        dve.wait_ge(dup_steps, q * STEPS + 1)
                        find_moved(dve, moved, dup, q).then_inc(dup_steps, 1)
                        for j in range(TABLES):
                            wait_past(dve, scattered[j], (q - 1) * 16)
                        dve.wait_ge(dup_steps, q * STEPS + 2)
                        find_index(dve, idx[k], moved, q).then_inc(idx_ready, 1)

                    paced(dve, NG, step)

                @block.gpsimd
                def _(pool):
                    def step(q, s):
                        pool.wait_ge(vals_ready, q + 1)
                        pool.wait_ge(idx_ready, q + 1)
                        for j in range(TABLES):
                            wait_past(pool, scattered[j], q * 16)
                            pool.sem_inc(pool_turns, 1)
                            scatter(pool, j, idx[s % 2], vals[s % 2], scattered)

                    paced(pool, NG, step)
                    for j in range(TABLES):
                        pool.wait_ge(scattered[j], NG * 16)

            with ExitStack() as ctx:
                done = sem("done_b", ctx)
                x_dst_ready = sem("x_dst_ready", ctx)
                hot_ready = sem("x_hot_ready", ctx)
                front_made = sem("x_front_made", ctx)
                hot_t_ready = sem("x_hot_t_ready", ctx)
                g_loaded = sem("x_g_loaded", ctx)
                rows_made = sem("x_rows_made", ctx)
                rows_kept = sem("x_rows_kept", ctx)
                same_ready = sem("x_same_ready", ctx)
                comb_made = sem("x_comb_made", ctx)
                vals_ready = sem("x_vals_ready", ctx)
                idx_ready = sem("x_idx_ready", ctx)
                dup_steps = sem("x_dup_steps", ctx)
                cnt_added = sem("x_cnt_added", ctx)
                scattered = [sem(f"x_scattered{j}", ctx) for j in range(TABLES)]
                turns = [sem(f"x_turns{n}", ctx) for n in range(4)]
                cnt_done = sem("cnt_done", ctx)
                cnt_saved = sem("cnt_saved", ctx)
                block = ctx.enter_context(nc.Block())
                STEPS = 2

                @block.sync
                def _(sp):
                    def extra(e, q, first, x):
                        sp.wait_ge(done, e + 1)
                        sp.sem_inc(turns[0], 1)
                        sp.dma_start(g_win[0][:, :], g_tab[bass.ds(first, P), :]).then_inc(g_loaded, 16)

                    each_extra(sp, extra)
                    sp.wait_ge(cnt_done, 1)
                    sp.dma_start(cnt_tab, cnt_acc[:, :]).then_inc(cnt_saved, 16)
                    sp.wait_ge(cnt_saved, 16)

                @block.scalar
                def _(act):
                    def extra(e, q, first, x):
                        act.wait_ge(front_made, e + 1)
                        act.copy(hot_t[:, :], t_ps[:, :]).then_inc(hot_t_ready, 1)
                        act.wait_ge(rows_made, e + 1)
                        act.copy(rows[:, :, :], rows_ps[:, :, :]).then_inc(rows_kept, 1)
                        act.wait_ge(comb_made, e + 1)
                        act.wait_ge(done, e + 1)
                        act.copy(vals[0][:, :, :], comb_ps[:, :, :]).then_inc(vals_ready, 1)

                    each_extra(act, extra)

                @block.tensor
                def _(pe):
                    def extra(e, q, first, x):
                        pe.wait_ge(hot_ready, e + 1)
                        pe.sem_inc(turns[1], 1)
                        transpose_hots(pe, t_ps, hot[0])
                        count_by_node(pe, cnt_ps, hot[0])
                        src_along_rows(pe, src_ps, q).then_inc(front_made, 1)
                        pe.wait_ge(hot_t_ready, e + 1)
                        pe.wait_ge(g_loaded, e * 16 + 16)
                        rows_by_dst(pe, rows_ps, hot_t, g_win[0]).then_inc(rows_made, 1)
                        pe.wait_ge(rows_kept, e + 1)
                        pe.wait_ge(same_ready, e + 1)
                        sum_same(pe, comb_ps, same[0], rows).then_inc(comb_made, 1)

                    each_extra(pe, extra)

                @block.vector
                def _(dve):
                    def extra(e, q, first, x):
                        dve.wait_ge(done, e + 1)
                        dve.tensor_scalar(x_dst[:, :], in_group(dst_rel, q), block_base[:, bass.ds(x + 1, 1)], None,
                                          ALU.subtract).then_inc(x_dst_ready, 1)
                        dve.wait_ge(x_dst_ready, e + 1)
                        one_hots(dve, hot[0], x_dst[:, :]).then_inc(hot_ready, 1)
                        dve.wait_ge(front_made, e + 1)
                        add_count(dve, cnt_acc, first, cnt_ps).then_inc(cnt_added, 1)
                        dve.wait_ge(cnt_added, e + 1)
                        find_same(dve, same[0], src_ps, q).then_inc(same_ready, 1)
                        dve.wait_ge(same_ready, e + 1)
                        dve.sem_inc(turns[2], 1)
                        find_dup(dve, junk, same[0], dup).then_inc(dup_steps, 1)
                        dve.wait_ge(dup_steps, e * STEPS + 1)
                        find_moved(dve, moved, dup, q).then_inc(dup_steps, 1)
                        dve.wait_ge(dup_steps, e * STEPS + 2)
                        find_index(dve, idx[0], moved, q).then_inc(idx_ready, 1)

                    each_extra(dve, extra)
                    dve.sem_inc(cnt_done, 1)

                @block.gpsimd
                def _(pool):
                    pool.sem_inc(done, 1)

                    def extra(e, q, first, x):
                        pool.wait_ge(vals_ready, e + 1)
                        pool.wait_ge(idx_ready, e + 1)
                        pool.sem_inc(turns[3], 1)
                        for j in range(TABLES):
                            scatter(pool, j, idx[0], vals[0], scattered)
                        for j in range(TABLES):
                            pool.wait_ge(scattered[j], e * 16 + 16)
                        pool.sem_inc(done, 1)

                    each_extra(pool, extra)

        nb2 = sb("nb2", [P, H], F32)
        b1_col = sb("b1_col", [H, 1], F32)
        w1c_sb = sb("w1c_sb", [P, H], F32)
        w2_sb = sb("w2_sb", [H, H], F32)
        w3_sb = sb("w3_sb", [H, F], F32)
        inv_cnt = sb("inv_cnt", [P, NB], F32)
        c_bc = sb("c_bc", [P, F], F32)
        seg_acc = sb("seg_acc", [H, NPP], F32)
        with ExitStack() as ctx:
            parts = [[sb(f"part{k}_{j}", [P, CB, F], F32, ctx) for j in range(TABLES)] for k in range(2)]
            agg = [sb(f"agg{k}", [P, CB, F], F32, ctx) for k in range(2)]
            h_blk = [sb(f"h_blk{k}", [P, CB, F], F32, ctx) for k in range(2)]
            p_out = [sb(f"p_out{k}", [P, CB, PLANES, H], BF16, ctx) for k in range(2)]
            q_out = [sb(f"q_out{k}", [P, CB, PLANES, H], BF16, ctx) for k in range(2)]
            w0_sb = sb("w0_sb", [F, F], F32, ctx)
            w1_sb = sb("w1_sb", [F, 2 * H], F32, ctx)
            b0_bc = sb("b0_bc", [P, F], F32, ctx)
            b3_bc = sb("b3_bc", [P, F], F32, ctx)
            cnt_rows = sb("cnt_rows", [NB, P], F32, ctx)
            b2_col = sb("b2_col", [H, 1], F32, ctx)
            agg_t = sb("agg_t", [F, CB, P], F32, ctx)
            h_t = sb("h_t", [F, CB, P], F32, ctx)
            y = sb("y", [P, CB, F], F32, ctx)
            dst_cnt = sb("dst_cnt", [P, NB], F32, ctx)
            has_edge = sb("has_edge", [P, NB], F32, ctx)
            constant = sb("constant", [P, CB, F], F32, ctx)
            y_h = sb("y_h", [P, CB, F], F32, ctx)
            squares = sb("squares_c", [P, CB, F], F32, ctx)
            rest = sb("rest", [P, CB, 2 * H], F32, ctx)
            t_ps = ps("t_ps_c", [F, 8, P], F32, ctx)
            y_ps = ps("y_ps", [P, CB, F], F32, ctx)
            pq_ps = ps("pq_ps", [P, 8, 2 * H], F32, ctx)
            c_ps = ps("c_ps", [P, F + NB], F32, ctx)

            parts_loaded = [[sem(f"part_loaded{k}_{j}", ctx) for j in range(TABLES)] for k in range(2)]
            w_loaded = sem("w_loaded", ctx)
            cnt_loaded = sem("cnt_loaded", ctx)
            w1c_zero = sem("w1c_zero", ctx)
            c_made = sem("c_made", ctx)
            chain = sem("chain_c", ctx)
            steps = sem("steps_c", ctx)
            summed = sem("summed", ctx)
            agg_ready = sem("agg_ready", ctx)
            agg_t_made = sem("agg_t_made", ctx)
            agg_t_ready = sem("agg_t_ready", ctx)
            y_made = sem("y_made", ctx)
            y_used = sem("y_used", ctx)
            var_ready = sem("var_ready", ctx)
            pow_done = sem("pow_done_c", ctx)
            h_ready = sem("h_ready", ctx)
            h_kept = sem("h_kept", ctx)
            h_t_made = sem("h_t_made", ctx)
            h_t_ready = sem("h_t_ready", ctx)
            pq_made = sem("pq_made", ctx)
            plane_ready = sem("plane_ready", ctx)
            rest_ready = sem("rest_ready", ctx)
            stored = [sem(f"planes_stored{k}", ctx) for k in range(2)]
            turns = sem("turns_c", ctx)
            turns_pool = sem("turns_pool_c", ctx)
            turns_pe = sem("turns_pe_c", ctx)
            turns_dve = sem("turns_dve_c", ctx)
            scaled = sem("scaled", ctx)
            c_kept = sem("c_kept", ctx)
            constant_ready = sem("constant_ready", ctx)
            x1_kept = sem("x1_kept", ctx)
            block = ctx.enter_context(nc.Block())
            W_LOADS = 10
            LAG = 4

            def live(k):
                return not isinstance(k, int) or 0 <= k < NK

            def blocks(k):
                return bass.ds(k * CB, CB)

            def landed(k, s):
                return (k - s) * 8 + 16

            @block.sync
            def _(sp):
                def load(k, s):
                    wait_past(sp, agg_ready, k - 1)
                    sp.sem_inc(turns, 1)
                    for j in range(TABLES):
                        sp.dma_start(parts[s][j][:, :, :], node_view(sum_tab[j])[:, blocks(k), :]
                                     ).then_inc(parts_loaded[s][j], 16)

                def weight(dst, src):
                    sp.dma_start(dst, src).then_inc(w_loaded, 16)

                for k in range(min(NK, 2)):
                    load(k, k)
                weight(w0_sb[:, :], w0_t)
                weight(w1_sb[:, :], w1ab)
                weight(w2_sb[:, :], w2)
                weight(w3_sb[:, :], w3)
                weight(b0_bc[:, :], b0.to_broadcast([P, F]))
                weight(b3_bc[:, :], b3.to_broadcast([P, F]))
                weight(nb2[:, :], b2.to_broadcast([P, H]))
                weight(b1_col[:, :], b1)
                weight(b2_col[:, :], b2.rearrange("o h -> h o"))
                sp.wait_ge(w1c_zero, 1)
                weight(w1c_sb[0:EF, :], w1c)
                sp.dma_start(cnt_rows[:, :], cnt_tab[0:1, 0:NP].rearrange("o (b p) -> (o b) p", p=P)
                             ).then_inc(cnt_loaded, 16)

                def turn(k, s):
                    if not isinstance(k, int) or k + 2 < NK:
                        load(k + 2, s)
                    if live(k - LAG):
                        n, o = k - LAG, s
                        sp.wait_ge(plane_ready, (n + 1) * PLANES)
                        sp.sem_inc(turns, 1)
                        for table, planes in ((p_tab, p_out[o]), (q_tab, q_out[o])):
                            sp.dma_start(node_view(table)[:, blocks(n), :],
                                         planes[:, :, :, :].rearrange("p b k h -> p b (k h)")).then_inc(stored[o], 16)

                lagged(sp, NK - 2, LAG + 2, turn)
                for k in range(2):
                    wait_past(sp, stored[k], (NK + 1 - k) // 2 * 32)

            @block.gpsimd
            def _(pool):
                pool.memset(w1c_sb[:, :], 0.0).then_inc(w1c_zero, 1)
                pool.memset(seg_acc[:, :], 0.0)

                def turn(k, s):
                    if live(k - 1):
                        n = k - 1
                        pool.wait_ge(var_ready, n + 1)
                        pool.sem_inc(turns_pool, 1)
                        pool.tensor_tensor(stat[:, blocks(n)], stat[:, blocks(n)], half[:, blocks(n)], ALU.pow
                                           ).then_inc(pow_done, 1)
                    if live(k - 2):
                        n = k - 2
                        pool.wait_ge(h_ready, n + 1)
                        pool.sem_inc(turns_pool, 1)
                        at, add = x1[:, blocks(n), :], constant[:, :, :]
                        wait_past(pool, x1_kept, n)
                        pool.sem_inc(turns_pool, 1)
                        pool.tensor_tensor(at, at, h_blk[s][:, :, :], ALU.add).then_inc(h_kept, 1)
                        pool.tensor_tensor(add, c_bc[:, :].unsqueeze(1).to_broadcast([P, CB, F]),
                                           has_edge[:, blocks(n)].unsqueeze(2).to_broadcast([P, CB, F]), ALU.mult
                                           ).then_inc(constant_ready, 1)
                        pool.wait_ge(constant_ready, n + 1)
                        pool.wait_ge(h_kept, n + 1)
                        pool.sem_inc(turns_pool, 1)
                        pool.tensor_tensor(at, at, add, ALU.add).then_inc(x1_kept, 1)

                pool.wait_ge(c_kept, 1)
                lagged(pool, NK, LAG, turn)
                pool.wait_ge(x1_kept, NK)

            @block.tensor
            def _(pe):
                pe.wait_ge(w_loaded, 16 * W_LOADS)
                pe.matmul(c_ps[:, 0:F], b2_col[:, 0:1].to_broadcast([H, P]), w3_sb[:, :], start=True,
                          stop=True)
                pe.wait_ge(cnt_loaded, 16)
                pe.transpose(c_ps[:, F:F + NB], cnt_rows[:, :], ident_f[0:NB, 0:NB]).then_inc(c_made, 1)

                def transposed(a):
                    for c in range(CB):
                        last = pe.transpose(t_ps[:, c, :], a[:, c, :], ident_f[:, :])
                    return last

                def turn(k, s):
                    if live(k):
                        pe.wait_ge(agg_ready, k + 1)
                        wait_past(pe, h_t_ready, k - 2)
                        pe.sem_inc(turns_pe, 1)
                        transposed(agg[s]).then_inc(agg_t_made, 1)
                    if live(k - 3):
                        n = k - 3
                        pe.wait_ge(h_t_ready, n + 1)
                        wait_past(pe, rest_ready, (n - 1) * 2 + 1)
                        pe.sem_inc(turns_pe, 1)
                        for c in range(CB):
                            last = pe.matmul(pq_ps[:, c, :], h_t[:, c, :], w1_sb[:, :], start=True, stop=True)
                        last.then_inc(pq_made, 1)
                    if live(k):
                        pe.wait_ge(agg_t_ready, k + 1)
                        wait_past(pe, y_used, k)
                        pe.sem_inc(turns_pe, 1)
                        for c in range(CB):
                            last = pe.matmul(y_ps[:, c, :], agg_t[:, c, :], w0_sb[:, :], start=True, stop=True)
                        last.then_inc(y_made, 1)
                    if live(k - 2):
                        pe.wait_ge(h_ready, k - 1)
                        pe.sem_inc(turns_pe, 1)
                        transposed(h_blk[s]).then_inc(h_t_made, 1)

                lagged(pe, NK, LAG, turn)

            @block.scalar
            def _(act):
                def round_planes(n, o, m):
                    v = pq_ps[:, 0:CB, :] if m == 0 else rest[:, :, :]
                    act.copy(p_out[o][:, :, m, :], v[:, :, 0:H])
                    act.copy(q_out[o][:, :, m, :], v[:, :, H:2 * H]).then_inc(plane_ready, 1)

                def turn(k, s):
                    if live(k):
                        wait_past(act, y_made, k)
                        act.wait_ge(agg_t_made, k + 1)
                        act.copy(agg_t[:, :, :], t_ps[:, 0:CB, :]).then_inc(agg_t_ready, 1)
                    if live(k - 4):
                        act.wait_ge(rest_ready, (k - 4) * 2 + 2)
                        round_planes(k - 4, s, 2)
                    n, o = k - 3, 1 - s
                    if live(n):
                        act.wait_ge(pq_made, n + 1)
                        wait_past(act, stored[o], (n - o) * 16)
                        round_planes(n, o, 0)
                    if live(k - 2):
                        act.wait_ge(h_t_made, k - 1)
                        act.copy(h_t[:, :, :], t_ps[:, 0:CB, :]).then_inc(h_t_ready, 1)
                    if live(n):
                        act.wait_ge(rest_ready, n * 2 + 1)
                        round_planes(n, o, 1)

                lagged(act, NK, LAG, turn)

            @block.vector
            def _(dve):
                link = linker(dve, chain)
                dve.wait_ge(w_loaded, 16 * W_LOADS)
                link(dve.tensor_scalar(nb2[:, :], nb2[:, :], -1.0, None, ALU.mult))
                dve.wait_ge(c_made, 1)
                dve.tensor_copy(dst_cnt[:, :], c_ps[:, F:F + NB])
                link(dve.tensor_tensor(c_bc[:, :], c_ps[:, 0:F], b3_bc[:, :], ALU.add))
                link(dve.tensor_scalar(inv_cnt[:, :], dst_cnt[:, :], 1.0, None, ALU.max))
                link(dve.reciprocal(inv_cnt[:, :], inv_cnt[:, :]))
                link(dve.tensor_scalar(has_edge[:, :], dst_cnt[:, :], 0.0, None, ALU.is_gt))
                dve.sem_inc(c_kept, 1)
                nodes = [P, CB, F]

                def stepper(base):
                    count = [0]

                    def link(ins):
                        count[0] += 1
                        ins.then_inc(steps, 1)
                        dve.wait_ge(steps, base + count[0])
                        dve.sem_inc(turns_dve, 1)
                    return link

                STEPS = 7

                def subtract_planes(n, o, m):
                    dve.wait_ge(plane_ready, n * PLANES + m + 1)
                    v = pq_ps[:, 0:CB, :] if m == 0 else rest[:, :, :]
                    for w, planes in ((0, p_out[o]), (1, q_out[o])):
                        last = dve.tensor_tensor(rest[:, :, w * H:(w + 1) * H], v[:, :, w * H:(w + 1) * H],
                                                 planes[:, :, m, :], ALU.subtract)
                    last.then_inc(rest_ready, 1)

                def turn(k, s):
                    if live(k):
                        total = parts[s][0]
                        for j in range(TABLES):
                            dve.wait_ge(parts_loaded[s][j], landed(k, s))
                            if j:
                                dve.tensor_tensor(total[:, :, :], total[:, :, :], parts[s][j][:, :, :], ALU.add
                                                  ).then_inc(summed, 1)
                                dve.wait_ge(summed, k * (TABLES - 1) + j)
                        wait_past(dve, agg_t_made, k - 1)
                        dve.tensor_tensor(agg[s][:, :, :], total[:, :, :],
                                          deg_is[:, blocks(k)].unsqueeze(2).to_broadcast(nodes),
                                          ALU.mult).then_inc(agg_ready, 1)
                    if live(k - 4):
                        subtract_planes(k - 4, s, 1)
                    if live(k - 1):
                        n = k - 1
                        link = stepper(n * STEPS)
                        dve.wait_ge(y_made, n + 1)
                        dve.tensor_tensor(y[:, :, :], y_ps[:, :, :], b0_bc[:, :].unsqueeze(1).to_broadcast(nodes),
                                          ALU.add).then_inc(y_used, 1)
                        dve.wait_ge(y_used, n + 1)
                        link(dve.scalar_tensor_tensor(x1[:, blocks(n), :], y[:, :, :], 0.0, x1[:, blocks(n), :],
                                                      ALU.max, ALU.add))
                        center(dve, link, x1[:, blocks(n), :], act_in[:, blocks(n), :], squares[:, :, :],
                               stat[:, blocks(n)])
                        dve.sem_inc(var_ready, 1)
                    if live(k - 2):
                        n = k - 2
                        dve.wait_ge(pow_done, n + 1)
                        wait_past(dve, h_t_made, n - 1)
                        wait_past(dve, h_kept, n - 1)
                        dve.tensor_tensor(y_h[:, :, :], act_in[:, blocks(n), :],
                                          stat[:, blocks(n)].unsqueeze(2).to_broadcast(nodes), ALU.mult
                                          ).then_inc(scaled, 1)
                        dve.wait_ge(scaled, n + 1)
                        dve.tensor_scalar(h_blk[s][:, :, :], y_h[:, :, :], 0.0, None, ALU.max).then_inc(h_ready, 1)
                    if live(k - 3):
                        subtract_planes(k - 3, 1 - s, 0)

                lagged(dve, NK, LAG, turn)

        def edge_part(pe, z1, ef):
            for k in range(2):
                pe.matmul(z1[k][:, 0:WH], w1c_sb[:, :], ef[:, k * WH:(k + 1) * WH], start=True, stop=False,
                          skip_group_check=True)

        def src_part(pe, z1, p_rows):
            for j in range(GROUP):
                for m in range(PLANES):
                    pe.matmul(z1[j // 2][:, (j % 2) * P:(j % 2 + 1) * P], p_rows[:, j, m * H:(m + 1) * H],
                              ident_b[:, :], start=False, stop=False, skip_group_check=True)

        def dst_part(pe, z1, k, q_win, hot_t):
            for m in range(PLANES):
                last = pe.matmul(z1[k][:, 0:WH], q_win[:, m * H:(m + 1) * H], hot_t[:, k * WH:(k + 1) * WH],
                                 start=False, stop=(m == PLANES - 1), skip_group_check=True)
            return last

        def second_layer(pe, z2, h1, k):
            for j in range(2):
                last = pe.matmul(z2[k][:, j, :], h1[:, k, j * P:(j + 1) * P], w2_sb[:, :], start=True, stop=True)
            return last

        def sum_by_node(pe, seg_ps, h2, hot):
            for j in range(GROUP):
                last = pe.matmul(seg_ps[:, :], h2[:, j, :], hot[:, j, :], start=(j == 0), stop=(j == GROUP - 1))
            return last

        def make_h1(act, h1, z1, k):
            return act.activation(h1[:, k, :], z1[k][:, 0:WH], ACT.Relu, bias=b1_col[:, 0:1])

        def make_h2(dve, h2, z2, k):
            return dve.tensor_tensor(h2[:, 2 * k:2 * k + 2, :], z2[k][:, 0:2, :],
                                     nb2[:, :].unsqueeze(1).to_broadcast([P, 2, H]), ALU.max)

        def add_seg(dve, first, seg_ps):
            at = seg_acc[:, bass.ds(first, P)]
            return dve.tensor_tensor(at, at, seg_ps[:, :], ALU.add)

        def gather(pool, p_rows, idx, landed):
            for j in range(GROUP):
                pool.indirect_dma_start(p_rows[:, j, :], None, p_tab, bass.IndirectOffsetOnAxis(idx[:, j:j + 1], 0)
                                        ).then_inc(landed, 16)

        with ExitStack() as life:
            idx = [sb(f"idx_d{s}", [P, GROUP], I32, life) for s in range(UNROLL)]
            p_got = [sb(f"p_got{s}", [P, GROUP, PLANES * H], BF16, life) for s in range(UNROLL)]
            q_win = [sb(f"q_win{k}", [P, PLANES * H], BF16, life) for k in range(2)]
            ef = [sb(f"ef{k}", [P, W], F32, life) for k in range(2)]
            hot = [sb(f"hot_d{k}", [P, GROUP, P], BF16, life) for k in range(2)]
            hot_t = sb("hot_t_d", [P, W], BF16, life)
            hot_f = [sb(f"hot_f{k}", [P, GROUP, P], F32, life) for k in range(2)]
            h1 = sb("h1", [H, 2, WH], F32, life)
            h2 = sb("h2", [P, GROUP, H], F32, life)
            x_dst = sb("x_dst_d", [P, GROUP], F32, life)
            t_ps = ps("t_ps_d", [P, W], BF16, life)
            z1 = [ps(f"z1_{k}", [H, 512], F32, life) for k in range(2)]
            z2 = [ps(f"z2_{k}", [P, 4, H], F32, life) for k in range(2)]
            seg_ps = ps("seg_ps", [H, P], F32, life)

            with ExitStack() as ctx:
                ef_zero = sem("ef_zero", ctx)
                ef_loaded = [sem(f"ef_loaded{k}", ctx) for k in range(2)]
                q_loaded = [sem(f"q_loaded{k}", ctx) for k in range(2)]
                idx_loaded = [sem(f"idx_loaded{s}", ctx) for s in range(UNROLL)]
                gathered = [sem(f"gathered{s}", ctx) for s in range(UNROLL)]
                hot_ready = sem("hot_ready_d", ctx)
                hot_f_ready = sem("hot_f_ready", ctx)
                t_made = sem("t_made_d", ctx)
                hot_t_ready = sem("hot_t_ready_d", ctx)
                z1_made = sem("z1_made", ctx)
                h1_ready = sem("h1_ready", ctx)
                z2_made = sem("z2_made", ctx)
                h2_ready = sem("h2_ready", ctx)
                seg_made = sem("seg_made", ctx)
                seg_added = sem("seg_added", ctx)
                sp_turns = sem("sp_turns_d", ctx)
                pool_turns = sem("pool_turns_d", ctx)
                pe_turns = sem("pe_turns_d", ctx)
                block = ctx.enter_context(nc.Block())

                @block.sync
                def _(sp):
                    def load_idx(q, s):
                        sp.dma_start(idx[s][:, :], in_group(src_col, q)).then_inc(idx_loaded[s], 16)

                    load_idx(0, 0)
                    load_idx(1, 1)
                    sp.wait_ge(ef_zero, 1)

                    def step(q, s):
                        wait_past(sp, z1_made, q * 2 - 2)
                        sp.sem_inc(sp_turns, 1)
                        if not isinstance(q, int) or q + 2 < NG:
                            load_idx(q + 2, (s + 2) % UNROLL)
                        k = s % 2
                        sp.dma_start(ef[k][0:EF, :], edge_t[:, bass.ds(q * W, W)]).then_inc(ef_loaded[k], 16)
                        base = load_base(sp, q)
                        sp.dma_start(q_win[k][:, :], q_tab[bass.ds(base, P), :]).then_inc(q_loaded[k], 16)

                    paced(sp, NG, step)

                @block.gpsimd
                def _(pool):
                    pool.memset(ef[0][:, :], 0.0)
                    pool.memset(ef[1][:, :], 0.0).then_inc(ef_zero, 1)

                    def step(q, s):
                        pool.wait_ge(idx_loaded[s], in_slot(q, s, UNROLL, 16))
                        pool.sem_inc(pool_turns, 1)
                        wait_past(pool, z1_made, (q - UNROLL + 1) * 2)
                        pool.sem_inc(pool_turns, 1)
                        gather(pool, p_got[s], idx[s], gathered[s])

                    paced(pool, NG, step)

                @block.scalar
                def _(act):
                    def step(q, s):
                        act.wait_ge(t_made, q + 1)
                        wait_past(act, z1_made, q * 2)
                        act.copy(hot_t[:, :], t_ps[:, :]).then_inc(hot_t_ready, 1)
                        wait_past(act, seg_made, q - 1)
                        act.copy(hot_f[s % 2][:, :, :], hot[s % 2][:, :, :]).then_inc(hot_f_ready, 1)
                        for k in range(2):
                            act.wait_ge(z1_made, q * 2 + (k + 1))
                            wait_past(act, z2_made, q * 2)
                            make_h1(act, h1, z1, k).then_inc(h1_ready, 1)

                    paced(act, NG, step)

                @block.tensor
                def _(pe):
                    def second(q):
                        for k in range(2):
                            pe.wait_ge(h1_ready, q * 2 + (k + 1))
                            wait_past(pe, h2_ready, q * 2 - 1 + k)
                            second_layer(pe, z2, h1, k).then_inc(z2_made, 1)

                    def segment(q, s):
                        pe.wait_ge(h2_ready, q * 2 + 2)
                        pe.wait_ge(hot_f_ready, q + 1)
                        wait_past(pe, seg_added, q)
                        sum_by_node(pe, seg_ps, h2, hot_f[s % 2]).then_inc(seg_made, 1)

                    def step(q, s):
                        k2 = s % 2
                        pe.wait_ge(hot_ready, q + 1)
                        pe.sem_inc(pe_turns, 1)
                        wait_past(pe, hot_t_ready, q)
                        pe.sem_inc(pe_turns, 1)
                        transpose_hots(pe, t_ps, hot[k2]).then_inc(t_made, 1)
                        wait_past(pe, h1_ready, q * 2)
                        pe.wait_ge(ef_loaded[k2], in_slot(q, s, 2, 16))
                        edge_part(pe, z1, ef[k2])
                        if not isinstance(q, int) or q > 0:
                            second(q - 1)
                        pe.wait_ge(gathered[s], in_slot(q, s, UNROLL, 16 * GROUP))
                        src_part(pe, z1, p_got[s])
                        pe.wait_ge(hot_t_ready, q + 1)
                        pe.wait_ge(q_loaded[k2], in_slot(q, s, 2, 16))
                        for k in range(2):
                            dst_part(pe, z1, k, q_win[k2], hot_t).then_inc(z1_made, 1)
                        if not isinstance(q, int) or q > 0:
                            segment(q - 1, s - 1)

                    paced(pe, NG, step)
                    second(NG - 1)
                    segment(NG - 1, UNROLL - 1)

                @block.vector
                def _(dve):
                    one_hots(dve, hot[0], in_group(dst_rel, 0)).then_inc(hot_ready, 1)

                    def keep_h2(q):
                        for k in range(2):
                            dve.wait_ge(z2_made, q * 2 + (k + 1))
                            wait_past(dve, seg_made, q)
                            make_h2(dve, h2, z2, k).then_inc(h2_ready, 1)

                    def add_segments(q):
                        dve.wait_ge(seg_made, q + 1)
                        wait_past(dve, seg_added, q)
                        add_seg(dve, load_base(dve, q), seg_ps).then_inc(seg_added, 1)

                    def step(q, s):
                        k = s % 2
                        if not isinstance(q, int) or q + 1 < NG:
                            wait_past(dve, t_made, q)
                            wait_past(dve, hot_f_ready, q)
                            one_hots(dve, hot[1 - k], in_group(dst_rel, q + 1)).then_inc(hot_ready, 1)
                        if not isinstance(q, int) or q > 0:
                            keep_h2(q - 1)
                            add_segments(q - 1)

                    paced(dve, NG, step)
                    keep_h2(NG - 1)
                    add_segments(NG - 1)

            with ExitStack() as ctx:
                done = sem("done_d", ctx)
                loaded = sem("xd_loaded", ctx)
                gathered = sem("xd_gathered", ctx)
                x_dst_ready = sem("xd_dst_ready", ctx)
                hot_ready = sem("xd_hot_ready", ctx)
                hot_f_ready = sem("xd_hot_f_ready", ctx)
                t_made = sem("xd_t_made", ctx)
                hot_t_ready = sem("xd_hot_t_ready", ctx)
                z1_made = sem("xd_z1_made", ctx)
                h1_ready = sem("xd_h1_ready", ctx)
                z2_made = sem("xd_z2_made", ctx)
                h2_ready = sem("xd_h2_ready", ctx)
                seg_made = sem("xd_seg_made", ctx)
                turns = [sem(f"xd_turns{n}", ctx) for n in range(3)]
                block = ctx.enter_context(nc.Block())
                LOADS = 3

                @block.sync
                def _(sp):
                    def extra(e, q, first, x):
                        sp.wait_ge(done, e + 1)
                        sp.sem_inc(turns[0], 1)
                        sp.dma_start(idx[0][:, :], in_group(src_col, q)).then_inc(loaded, 16)
                        sp.dma_start(ef[0][0:EF, :], edge_t[:, bass.ds(q * W, W)]).then_inc(loaded, 16)
                        sp.dma_start(q_win[0][:, :], q_tab[bass.ds(first, P), :]).then_inc(loaded, 16)

                    each_extra(sp, extra)

                @block.gpsimd
                def _(pool):
                    def extra(e, q, first, x):
                        pool.wait_ge(loaded, (e + 1) * (LOADS * 16))
                        pool.sem_inc(turns[1], 1)
                        gather(pool, p_got[0], idx[0], gathered)

                    each_extra(pool, extra)

                @block.scalar
                def _(act):
                    def extra(e, q, first, x):
                        act.wait_ge(t_made, e + 1)
                        act.copy(hot_t[:, :], t_ps[:, :]).then_inc(hot_t_ready, 1)
                        act.copy(hot_f[0][:, :, :], hot[0][:, :, :]).then_inc(hot_f_ready, 1)
                        act.wait_ge(z1_made, e + 1)
                        make_h1(act, h1, z1, 0)
                        make_h1(act, h1, z1, 1).then_inc(h1_ready, 1)

                    each_extra(act, extra)

                @block.tensor
                def _(pe):
                    def extra(e, q, first, x):
                        pe.wait_ge(hot_ready, e + 1)
                        pe.sem_inc(turns[2], 1)
                        transpose_hots(pe, t_ps, hot[0]).then_inc(t_made, 1)
                        pe.wait_ge(loaded, (e + 1) * (LOADS * 16))
                        edge_part(pe, z1, ef[0])
                        pe.wait_ge(gathered, (e + 1) * (GROUP * 16))
                        src_part(pe, z1, p_got[0])
                        pe.wait_ge(hot_t_ready, e + 1)
                        dst_part(pe, z1, 0, q_win[0], hot_t)
                        dst_part(pe, z1, 1, q_win[0], hot_t).then_inc(z1_made, 1)
                        pe.wait_ge(h1_ready, e + 1)
                        second_layer(pe, z2, h1, 0)
                        second_layer(pe, z2, h1, 1).then_inc(z2_made, 1)
                        pe.wait_ge(h2_ready, e + 1)
                        pe.wait_ge(hot_f_ready, e + 1)
                        sum_by_node(pe, seg_ps, h2, hot_f[0]).then_inc(seg_made, 1)

                    each_extra(pe, extra)

                @block.vector
                def _(dve):
                    dve.sem_inc(done, 1)

                    def extra(e, q, first, x):
                        dve.wait_ge(done, e + 1)
                        dve.tensor_scalar(x_dst[:, :], in_group(dst_rel, q), block_base[:, bass.ds(x + 1, 1)], None,
                                          ALU.subtract).then_inc(x_dst_ready, 1)
                        dve.wait_ge(x_dst_ready, e + 1)
                        one_hots(dve, hot[0], x_dst[:, :]).then_inc(hot_ready, 1)
                        dve.wait_ge(z2_made, e + 1)
                        make_h2(dve, h2, z2, 0)
                        make_h2(dve, h2, z2, 1).then_inc(h2_ready, 1)
                        dve.wait_ge(seg_made, e + 1)
                        add_seg(dve, first, seg_ps).then_inc(done, 1)

                    each_extra(dve, extra)

        with ExitStack() as ctx:
            mean = [sb(f"mean{k}", [P, CB, F], F32, ctx) for k in range(2)]
            m_ps = [ps(f"m_ps{k}", [P, CB, F], F32, ctx) for k in range(2)]
            m_made = sem("m_made", ctx)
            mean_ready = sem("mean_ready", ctx)
            added = sem("added", ctx)
            stored = sem("stored", ctx)
            block = ctx.enter_context(nc.Block())

            @block.tensor
            def _(pe):
                for n in range(NK):
                    wait_past(pe, mean_ready, n - 1)
                    for c in range(CB):
                        at = (n * CB + c) * P
                        last = pe.matmul(m_ps[n % 2][:, c, :], seg_acc[:, at:at + P], w3_sb[:, :],
                                         start=True, stop=True)
                    last.then_inc(m_made, 1)

            @block.vector
            def _(dve):
                for n in range(NK):
                    part = slice(n * CB, (n + 1) * CB)
                    dve.wait_ge(m_made, n + 1)
                    dve.tensor_tensor(mean[n % 2][:, :, :], m_ps[n % 2][:, :, :],
                                      inv_cnt[:, part].unsqueeze(2).to_broadcast([P, CB, F]), ALU.mult
                                      ).then_inc(mean_ready, 1)
                    dve.wait_ge(mean_ready, n + 1)
                    dve.tensor_tensor(x1[:, part, :], x1[:, part, :], mean[n % 2][:, :, :], ALU.add
                                      ).then_inc(added, 1)

            @block.sync
            def _(sp):
                stores = 0
                for n in range(NK):
                    low, high = n * CB, (n + 1) * CB
                    whole_blocks = min(high, N // P)
                    sp.wait_ge(added, n + 1)
                    if whole_blocks > low:
                        stores += 1
                        sp.dma_start(out[low * P:whole_blocks * P, :].rearrange("(b p) f -> p b f", p=P),
                                     x1[:, low:whole_blocks, :]).then_inc(stored, 16)
                    if high * P > N:
                        stores += 1
                        sp.dma_start(out[whole_blocks * P:N, :], x1[0:N % P, whole_blocks, :]).then_inc(stored, 16)
                sp.wait_ge(stored, 16 * stores)


def layout(x, src, dst, edge_attr_16, L0_gnn_W, L0_gnn_b, L1_gnn_W1, L1_gnn_b1, L1_gnn_W2, L1_gnn_b2, L1_gnn_W3,
           L1_gnn_b3):
    import numpy as np

    def a(v):
        return np.ascontiguousarray(v)

    n, f = x.shape
    e, ef = edge_attr_16.shape
    padded = GROUP * UNROLL * -(-e // (P * GROUP * UNROLL))
    more = padded * P - e
    h = L1_gnn_W2.shape[0]
    src_p = np.concatenate([src, np.full(more, n + -n % P, src.dtype)])
    dst_p = np.concatenate([dst, np.full(more, PAD_NODE, dst.dtype)])
    w1 = np.asarray(L1_gnn_W1)
    return {
        "x": a(np.concatenate([x, np.zeros((-n % P, f), x.dtype)])),
        "src_col": a(src_p.reshape(padded, P).T),
        "dst_col": a(dst_p.reshape(padded, P).T),
        "dst_row": a(dst_p.reshape(padded // GROUP, GROUP * P)),
        "edge_t": a(np.concatenate([edge_attr_16, np.zeros((more, ef), edge_attr_16.dtype)]).T),
        "w0_t": a(np.asarray(L0_gnn_W).T),
        "b0": a(np.asarray(L0_gnn_b).reshape(1, f)),
        "w1ab": a(np.concatenate([w1[0:f], w1[f:2 * f]], axis=1)),
        "w1c": a(w1[2 * f:]),
        "b1": a(np.asarray(L1_gnn_b1).reshape(h, 1)),
        "w2": a(L1_gnn_W2),
        "b2": a(np.asarray(L1_gnn_b2).reshape(1, h)),
        "w3": a(L1_gnn_W3),
        "b3": a(np.asarray(L1_gnn_b3).reshape(1, f)),
    }


def kernel(**inputs):
    import numpy as np
    import concourse.bacc as bacc
    from concourse.bass_utils import run_bass_kernel_spmd

    inputs = {k: np.asarray(v) for k, v in inputs.items()}
    nc = bacc.Bacc("TRN2", target_bir_lowering=False, num_devices=1)
    arrays = layout(**inputs)
    args = [nc.dram_tensor(f"in_{k}", v.shape, mybir.dt.from_np(v.dtype), kind="ExternalInput").ap()
            for k, v in arrays.items()]
    out = nc.dram_tensor("out_0", inputs["x"].shape, F32, kind="ExternalOutput").ap()
    build_gnn(nc, *args, out)
    r = run_bass_kernel_spmd(nc, [{f"in_{k}": v for k, v in arrays.items()}], core_ids=[0])
    return r.results[0]["out_0"]
```
